# Optimizing a Trainium2 kernel written in Bass

```python
import numpy as np
import jax
import jax.numpy as jnp

def _softmax(x, axis=-1):
    return jax.nn.softmax(x, axis=axis)

def _gelu(x):
    return jax.nn.gelu(x, approximate=True)

def _silu(x):
    return jax.nn.silu(x)

def _sigmoid(x):
    return jax.nn.sigmoid(x)

def _layernorm(x, axis=-1, eps=1e-05):
    m = jnp.mean(x, axis=axis, keepdims=True)
    v = jnp.var(x, axis=axis, keepdims=True)
    return (x - m) / jnp.sqrt(v + eps)

def _scatter_add(tgt, idx, src, axis=0):
    return tgt.at[idx].add(src)

def _segment_sum(src, seg, n):
    return jax.ops.segment_sum(src, seg, n)
kernel_name = 'mk_adj_preln_d4_adj_r2_7f5823'

def setup_inputs(seed: int=0):
    np.random.seed(seed)
    _w = jnp.asarray

    def _rec_inputs():
        import jax
        import jax.numpy as jnp
        _gk = jax.random.key(seed)
        x = -0.000929 + 1 * jax.random.normal(jax.random.fold_in(_gk, 1), (4096, 128), jnp.float32)
        _w = (1.0 + jnp.arange(4096, dtype=jnp.float32)) ** (-0.5)
        _w = _w / _w.mean()
        _pij = jnp.clip(0.00195312 * _w[:, None] * _w[None, :], 0.0, 1.0)
        _a = jax.random.uniform(jax.random.fold_in(_gk, 2), (4096, 4096)) < _pij
        _a = jnp.logical_or(_a, jnp.eye(4096, dtype=bool))
        _af = _a.astype(jnp.float32)
        adj = _af
        return (x, adj)
    x, adj = _rec_inputs()

    def _L0_gnn_setup():
        import jax, jax.numpy as jnp
        import numpy as np
        N = 4096
        F_IN = 128
        F_OUT = 128
        BLOCK = 64

        def _graph_pool(out, adj):
            neg = jnp.asarray(jnp.finfo(out.dtype).min, out.dtype)

            def body(_, adj_blk):
                masked = jnp.where(adj_blk[:, :, None] != 0, out[None, :, :], neg)
                return (None, jnp.max(masked, axis=1))
            _, blocks = jax.lax.scan(body, None, adj.reshape(N // BLOCK, BLOCK, N))
            return blocks.reshape(N, out.shape[-1])
        key = jax.random.key(seed)
        k_in, k_adj, k_w, k_b = jax.random.split(key, 4)
        x = jax.random.normal(k_in, (N, F_IN), dtype=jnp.float32)
        adj = (jax.random.uniform(k_adj, (N, N)) < 0.01).astype(jnp.float32)
        adj = adj.at[jnp.arange(N), jnp.arange(N)].set(1.0)
        stdv = 1.0 / np.sqrt(F_OUT)
        weight = jax.random.uniform(k_w, (F_IN, F_OUT), minval=-stdv, maxval=stdv, dtype=jnp.float32)
        bias = jax.random.uniform(k_b, (F_OUT,), minval=-stdv, maxval=stdv, dtype=jnp.float32)
        return {'input': x, 'adj': adj, 'weight': weight, 'bias': bias}
    _L0_gnn_all = _L0_gnn_setup()
    _L0_gnn_in = {k: v for k, v in _L0_gnn_all.items() if k in ('weight', 'bias')}
    del _L0_gnn_all

    def _L1_gnn_setup():
        import jax, jax.numpy as jnp
        import numpy as np
        N = 4096
        D = 128
        EDGE_P = 0.005
        key = jax.random.key(seed)
        kx, ka, kb = jax.random.split(key, 3)
        x = jax.random.normal(kx, (N, D), dtype=jnp.float32)
        adj = (jax.random.uniform(ka, (N, N)) < EDGE_P).astype(jnp.float32)
        adj = jnp.maximum(adj, jnp.eye(N, dtype=jnp.float32))
        beta = jax.random.uniform(kb, (1,), dtype=jnp.float32)
        return {'x': x, 'adj': adj, 'beta': beta}
    _L1_gnn_all = _L1_gnn_setup()
    _L1_gnn_in = {k: v for k, v in _L1_gnn_all.items() if k in ('beta',)}
    del _L1_gnn_all

    def _L2_gnn_setup():
        import jax, jax.numpy as jnp
        import numpy as np
        N = 4096
        IN_DIM = 128
        OUT_DIM = 128
        key = jax.random.key(seed)
        k1, k2, k3, k4 = jax.random.split(key, 4)
        X = jax.random.normal(k1, (N, IN_DIM), dtype=jnp.float32)
        A = jax.random.uniform(k2, (N, N), dtype=jnp.float32)
        W = jax.random.normal(k3, (OUT_DIM, IN_DIM), dtype=jnp.float32) * (1.0 / np.sqrt(IN_DIM))
        b = jax.random.normal(k4, (OUT_DIM,), dtype=jnp.float32) * 0.01
        return {'X': X, 'A': A, 'W': W, 'b': b}
    _L2_gnn_all = _L2_gnn_setup()
    _L2_gnn_in = {k: v for k, v in _L2_gnn_all.items() if k in ('W', 'b')}
    del _L2_gnn_all

    def _L3_gnn_setup():
        import jax, jax.numpy as jnp
        import numpy as np
        N = 4096
        DIN = 128
        F = 64
        H = 2
        NEG_BIG = -10000000000.0
        key = jax.random.key(seed)
        k1, k2, k3, k4 = jax.random.split(key, 4)
        x = jax.random.normal(k1, (N, DIN), dtype=jnp.float32)
        adj = (jax.random.uniform(k2, (N, N)) < 0.002).astype(jnp.float32)
        idx = jnp.arange(N)
        adj = adj.at[idx, idx].set(1.0)
        kernels = jax.random.normal(k3, (H, DIN, F), dtype=jnp.float32) * 0.05
        att_kernels = jax.random.normal(k4, (H, 2 * F), dtype=jnp.float32) * 0.05
        return {'x': x, 'adj': adj, 'kernels': kernels, 'att_kernels': att_kernels}
    _L3_gnn_all = _L3_gnn_setup()
    _L3_gnn_in = {k: v for k, v in _L3_gnn_all.items() if k in ('kernels', 'att_kernels')}
    del _L3_gnn_all
    return {'x': x, 'adj': adj, 'L0_gnn_weight': _L0_gnn_in['weight'], 'L0_gnn_bias': _L0_gnn_in['bias'], 'L1_gnn_beta': _L1_gnn_in['beta'], 'L2_gnn_W': _L2_gnn_in['W'], 'L2_gnn_b': _L2_gnn_in['b'], 'L3_gnn_kernels': _L3_gnn_in['kernels'], 'L3_gnn_att_kernels': _L3_gnn_in['att_kernels']}

def reference(x, adj, L0_gnn_weight, L0_gnn_bias, L1_gnn_beta, L2_gnn_W, L2_gnn_b, L3_gnn_kernels, L3_gnn_att_kernels):
    import jax
    import jax.numpy as jnp

    def _L0_gnn_ref(input, adj, weight, bias):
        import jax, jax.numpy as jnp
        import numpy as np
        N = 4096
        F_IN = 128
        F_OUT = 128
        BLOCK = 64

        def _graph_pool(out, adj):
            neg = jnp.asarray(jnp.finfo(out.dtype).min, out.dtype)

            def body(_, adj_blk):
                masked = jnp.where(adj_blk[:, :, None] != 0, out[None, :, :], neg)
                return (None, jnp.max(masked, axis=1))
            _, blocks = jax.lax.scan(body, None, adj.reshape(N // BLOCK, BLOCK, N))
            return blocks.reshape(N, out.shape[-1])
        h = input @ weight
        out = jnp.maximum(adj @ h + bias, 0.0)
        return _graph_pool(out, adj)

    def _L1_gnn_ref(x, adj, beta):
        import jax, jax.numpy as jnp
        import numpy as np
        N = 4096
        D = 128
        EDGE_P = 0.005
        norm2 = jnp.linalg.norm(x, axis=1, keepdims=True)
        cos = beta[0] * (x @ x.T) / (norm2 @ norm2.T + 1e-07)
        masked = cos + (1.0 - adj) * -1000000000.0
        P = jax.nn.softmax(masked, axis=1)
        return P @ x

    def _L2_gnn_ref(X, A, W, b):
        import jax, jax.numpy as jnp
        import numpy as np
        N = 4096
        IN_DIM = 128
        OUT_DIM = 128
        n = A.shape[0]
        A_tilde = A + jnp.eye(n, dtype=A.dtype)
        deg = jnp.clip(A_tilde.sum(axis=1), 1e-12, None)
        d_inv_sqrt = deg ** (-0.5)
        A_norm = d_inv_sqrt[:, None] * A_tilde * d_inv_sqrt[None, :]
        h = A_norm @ X
        out = h @ W.T + b
        return jax.nn.relu(out)

    def _L3_gnn_ref(x, adj, kernels, att_kernels):
        import jax, jax.numpy as jnp
        import numpy as np
        N = 4096
        DIN = 128
        F = 64
        H = 2
        NEG_BIG = -10000000000.0
        conv = jnp.einsum('nd,hdf->hnf', x, kernels)
        a_self = jnp.einsum('hnf,hf->hn', conv, att_kernels[:, :F])
        a_neigh = jnp.einsum('hnf,hf->hn', conv, att_kernels[:, F:])
        scores = jax.nn.elu(a_self[:, :, None] + a_neigh[:, None, :], alpha=1.0)
        mask = jnp.exp(adj * NEG_BIG) * NEG_BIG
        p = jax.nn.softmax(scores + mask[None, :, :], axis=-1)
        out = jnp.einsum('hnm,hmf->hnf', p, conv)
        return out.transpose(1, 0, 2).reshape(N, H * F)
    h = jnp.maximum(_layernorm(x, axis=-1), 0.0)
    x = x + _L0_gnn_ref(h, adj, L0_gnn_weight, L0_gnn_bias)
    h = jnp.maximum(_layernorm(x, axis=-1), 0.0)
    x = x + _L1_gnn_ref(h, adj, L1_gnn_beta)
    h = jnp.maximum(_layernorm(x, axis=-1), 0.0)
    x = x + _L2_gnn_ref(h, adj, L2_gnn_W, L2_gnn_b)
    h = jnp.maximum(_layernorm(x, axis=-1), 0.0)
    x = x + _L3_gnn_ref(h, adj, L3_gnn_kernels, L3_gnn_att_kernels)
    return x

_drawn_inputs = setup_inputs


def setup_inputs(seed=0):
    import zlib

    import numpy as np

    out = dict(_drawn_inputs(seed))
    spreads = {}
    factors = {'L0_gnn_bias': 8.0, 'L2_gnn_b': 64.0, 'L3_gnn_att_kernels': 64.0}
    for name, (base, spread) in spreads.items():
        noise = np.random.default_rng([zlib.crc32(name.encode()), seed]).standard_normal(out[name].shape)
        drawn = base * np.exp(spread * noise) if base else spread * noise
        out[name] = jnp.asarray(drawn.astype(out[name].dtype))
    for name, factor in factors.items():
        out[name] = (out[name] * factor).astype(out[name].dtype)
    return out
```

```python
from contextlib import ExitStack

import concourse.bass as bass
from concourse import mybir

P = 128
F = 128
N = 4096
T = N // P
HEADS = 2
FH = F // HEADS
NB = 512
J = N // NB
GRID = P // HEADS
LN_EPS = 1e-5
COS_EPS = 1e-7
F32_MIN = -3.4028234663852886e38

ALU = mybir.AluOpType
ACT = mybir.ActivationFunctionType
F32 = mybir.dt.float32
BF16 = mybir.dt.bfloat16
FP8 = mybir.dt.float8e4
I32 = mybir.dt.int32
U8 = mybir.dt.uint8
AX_X = mybir.AxisListType.X
RMAX = bass.bass_isa.ReduceOp.max



class Tally:

    def __init__(self, sem):
        self.sem, self.n = sem, 0

    def up(self, ins):
        ins.then_inc(self.sem, 1)
        self.n = self.n + 1
        return ins

    def wait(self, eng):
        eng.wait_ge(self.sem, self.n)


class looped:

    def __init__(self, eng, count, *tallies):
        self.eng, self.count, self.tallies = eng, count, tallies

    def __enter__(self):
        self.cm = self.eng.Fori(0, self.count)
        i = self.cm.__enter__()
        self.base = [t.n for t, _ in self.tallies]
        for (t, per), b in zip(self.tallies, self.base):
            t.n = i * per + b
        return i

    def __exit__(self, *exc):
        r = self.cm.__exit__(*exc)
        for (t, per), b in zip(self.tallies, self.base):
            t.n = b + self.count * per
        return r


def build(nc, x, adj_t, w0, b0, beta, w2t, b2, k3, att, out):
    with ExitStack() as ctx:
        def sb(name, shape, dt):
            return ctx.enter_context(nc.sbuf_tensor(name, shape, dt))

        sems = {}

        def sem(name):
            if name not in sems:
                sems[name] = ctx.enter_context(nc.semaphore(name))
            return sems[name]

        table = nc.dram_tensor("v_table", (N, F), F32).ap()
        deg_dram = nc.dram_tensor("deg_rows", (N,), F32).ap()

        adj8 = sb("adj8", [P, T, N], FP8)
        ONE8 = 56.0
        adj_u8 = adj8[:].bitcast(U8)
        arena = sb("arena", [P, 73984 // 4], F32)

        def view(at, nbytes, dt):
            v = arena[:, at // 4:(at + nbytes) // 4]
            return v if dt == F32 else v.bitcast(dt)

        SPLIT_W = 3 * F + 2
        x0 = view(0, 16384, F32).rearrange("p (i f) -> p i f", f=F)
        ht0 = view(24704, 16384, F32)
        gs = view(0, 24704, BF16).rearrange("p (t c) -> p t c", c=SPLIT_W)
        ring0 = view(41088, 8192, F32).rearrange("p (b c) -> p b c", c=NB)
        STAGES, TQ, NQ = 4, 4, 256
        stage = view(49408, 16384, F32).rearrange("p (s t n) -> p s t n", s=STAGES, n=NQ)
        vring = view(24704, 1024, F32).rearrange("p (b f) -> p b f", b=2)
        xr = view(0, 16384, F32).rearrange("p (i f) -> p i f", f=F)
        ht = view(16384, 16384, F32)
        tp = view(32768, 16384, F32).rearrange("p (t f) -> p t f", f=F)
        dt_ = view(32768, 16384, F32)
        hp = view(32768, 16640, F32).rearrange("p (t c) -> p t c", c=130)
        gs2 = view(32768, 24704, BF16).rearrange("p (t c) -> p t c", c=SPLIT_W)
        vt = view(49408, 16384, F32)
        norm_bc = view(49408, 16384, F32)
        work = view(65792, 8192, F32).rearrange("p (b c) -> p b c", c=NB)
        junk = view(65792, 8192, BF16)[:, 0:2048]
        over_j = sb("over_j", [P, NB], BF16)[:]
        ind = view(49408, 4096, FP8).rearrange("p (t k) -> p t k", k=P)
        rows = view(53504, 12288, F32).rearrange("p (r h n) -> p r h n", r=3, n=NB)

        ident = sb("ident", [P, P], F32)
        ident_bf = sb("ident_bf", [P, P], BF16)
        ones = sb("ones", [P, P], F32)
        w0s = sb("w0s", [P, F], F32)
        w2s = sb("w2s", [P, F], F32)
        b0s = sb("b0s", [P, F], F32)
        b2s = sb("b2s", [P, F], F32)
        k3s = sb("k3s", [P, F + 2], F32)
        small = sb("small", [P, 512], F32)
        stats = small[:, 0:192].rearrange("p (i c) -> p i c", c=6)
        mv = small[:, 192:256].rearrange("p (i c) -> p i c", c=2)
        rstd = small[:, 256:288]
        degs = small[:, 288:320]
        degp = small[:, 320:352]
        none = small[:, 352:384]
        normp = small[:, 384:416]
        misc = small[:, 416:512]
        eps_col = misc[:, 0:1]
        beta_col = misc[:, 1:2]
        nbeta = misc[:, 2:3]
        rowmax = misc[:, 3:4]
        rinv = misc[:, 4:8]
        zero_col = misc[:, 8:9]
        rowmax2 = misc[:, 27:28]
        trange = misc[:, 9:17]
        tstep = misc[:, 17:19]
        tmin = misc[:, 19:21]
        rinv2 = misc[:, 21:25]
        s_col = misc[:, 25:27]
        tneigh = sb("tneigh", [P, T * HEADS], F32)[:].rearrange("p (t h) -> p t h", h=HEADS)
        column = sb("column", [P, 2, T], BF16)
        grid = sb("grid", [P, GRID], F32)
        over_raw = view(53504, 4096, U8)
        over = view(49408, 4096, U8)
        s_w = [w0s[:], w2s[:]]
        head_ones = b0s[:].bitcast(BF16).rearrange("p (h m) -> p h m", h=HEADS)
        theta = b2s[:].rearrange("p (h k) -> p h k", h=HEADS)
        cp = view(32768, 16640, F32).rearrange("p (t h c) -> p t h c", h=HEADS, c=FH + 1)

        ps = ctx.enter_context(nc.psum_tensor("ps", [P, 8, NB], F32))

        x_rows = x.rearrange("(i q) f -> q i f", q=P)
        out_rows = out.rearrange("(i q) f -> q i f", q=P)
        adj_spread = adj_t.rearrange("(p t) n -> p t n", p=P)

        def spread(a, t, k=1):
            v = a.rearrange("f (p t) -> f t p", t=T)
            if isinstance(t, int) and k == 1:
                return v[:, t, :]
            return v[:, bass.ds(t, k), :].rearrange("f o p -> f (o p)")

        QB = N // NQ
        QT = T // TQ
        HB = 4 * NB

        block = ctx.enter_context(nc.Block())

        def wait_reg(eng, s, value):
            eng.wait_ge(s, value)
            eng.sem_inc(sem("waits_passed"), 1)

        def tile(a, i):
            return a[:, bass.ds(i, 1), :].rearrange("p o f -> p (o f)")

        def col(a, i):
            return a[:, bass.ds(i, 1)]

        def blk(a, j, w=NB):
            return a[:, bass.ds(j * w, w)]

        @block.sync
        def _(sp):
            sp.dma_start(x0, x_rows).then_inc(sem("x0_in"), 16)
            for dst, src in ((w0s[:], w0), (w2s[:], w2t),
                             (k3s[:, 0:F].rearrange("p (h f) -> p h f", h=HEADS), k3.rearrange("h d f -> d h f")),
                             (b0s[:], b0.partition_broadcast(P)), (b2s[:], b2.partition_broadcast(P)),
                             (beta_col, beta.partition_broadcast(P))):
                sp.dma_start(dst, src).then_inc(sem("w_in"), 16)
            with sp.Fori(0, QB) as b:
                for q in range(QT):
                    sp.wait_ge(sem("cast"), b * QT + q + 1)
                    sp.dma_start(stage[:, q % STAGES], adj_spread[:, q * TQ:(q + 1) * TQ, bass.ds(b * NQ, NQ)]
                                 ).then_inc(sem(f"adj_in{q % STAGES}"), 16)
            sp.wait_ge(sem("agg0"), T)
            sp.dma_start(xr, x_rows).then_inc(sem("xr_in"), 16)
            sp.wait_ge(sem("agg0_used"), 2 + T)
            with nc.allow_non_contiguous_dma(reason="one word per node, once"):
                sp.dma_start(deg_dram.rearrange("(i q) -> q i", q=P), degs).then_inc(sem("deg_out"), 16)
            sp.wait_ge(sem("deg_out"), 16)
            sp.dma_start(degp, deg_dram.rearrange("(p t) -> p t", p=P)).then_inc(sem("deg_in"), 16)
            for u in range(2):
                sp.wait_ge(sem(f"v_stored{u}"), 16 * (T // 2))
            sp.dma_start(tp, table.rearrange("(p t) f -> p t f", p=P)).then_inc(sem("tp_in"), 16)
            sp.wait_ge(sem("x2"), 1)
            sp.dma_start(work[:, 0, 0:HEADS * F], att.rearrange("h f -> (h f)").partition_broadcast(P)
                         ).then_inc(sem("att_in"), 16)
            sp.wait_ge(sem("x3"), 1)
            sp.dma_start(out_rows, xr).then_inc(sem("out_stored"), 16)
            sp.wait_ge(sem("out_stored"), 16)

        def dve_front(dve, c, tag, src, ring):
            c.wait(dve)
            for i in range(T):
                c.up(nc.vector.bn_stats(stats[:, i, :], src[:, i, :]))
            c.wait(dve)
            for i in range(T):
                c.up(nc.vector.bn_aggr(mv[:, i, :], stats[:, i, :]))
            c.wait(dve)
            nc.vector.memset(eps_col, LN_EPS).then_inc(sem("var" + tag), 1)
            dve.wait_ge(sem("std" + tag), 1)
            c.up(nc.vector.reciprocal(rstd, rstd))
            c.wait(dve)
            with dve.Fori(0, J // 2) as g2:
                for u in range(2):
                    dve.wait_ge(sem("yt" + tag), g2 * 2 + u + 1)
                    for k in range(4):
                        i = g2 * 8 + u * 4 + k
                        ins = nc.vector.tensor_scalar(ring[:, u, k * F:(k + 1) * F], tile(src, i),
                                                      tile(mv, i)[:, 0:1], col(rstd, i), ALU.subtract, ALU.mult)
                    ins.then_inc(sem("y" + tag), 1)

        def pe_front(pe, tag, ring):
            pe.sem_inc(sem("yt" + tag), 2)
            with pe.Fori(0, J // 2) as g2:
                for u in range(2):
                    pe.wait_ge(sem("y" + tag), g2 * 2 + u + 1)
                    pe.wait_ge(sem("ht" + tag), g2 * 2 + u + 1)
                    for k in range(4):
                        ins = nc.tensor.transpose(ps[:, u, k * F:(k + 1) * F], ring[:, u, k * F:(k + 1) * F], ident[:])
                    ins.then_inc(sem("yt" + tag), 1)

        def act_front(act, tag, dst):
            act.sem_inc(sem("ht" + tag), 2)
            act.wait_ge(sem("var" + tag), 1)
            nc.scalar.activation(rstd, mv[:, :, 1], ACT.Sqrt, bias=eps_col).then_inc(sem("std" + tag), 1)
            with act.Fori(0, J // 2) as g2:
                for u in range(2):
                    act.wait_ge(sem("yt" + tag), g2 * 2 + u + 3)
                    nc.scalar.activation(blk(dst, g2 * 2 + u), ps[:, u, :], ACT.Relu).then_inc(sem("ht" + tag), 1)

        def pe_features(pe, tag, h, w):
            pe.wait_ge(sem("ht" + tag), 2 + J)
            for g2 in range(J // 2):
                for u in range(2):
                    pe.wait_ge(sem("g_read" + tag), g2 * 2 + u + 1)
                    for k in range(4):
                        ins = nc.tensor.matmul(ps[:, 2 + u, k * F:(k + 1) * F], spread(h, g2 * 8 + u * 4 + k), w,
                                               start=True, stop=True)
                    ins.then_inc(sem("g" + tag), 1)

        def act_features(act, tag, ring, dst):
            with act.Fori(0, J // 2) as g2:
                for u in range(2):
                    act.wait_ge(sem("g_read" + tag), g2 * 2 + u + 3)
                    nc.scalar.activation(dst[:, bass.ds(g2 * 8 + u * 4, 4), 0:F],
                                         ring[:, u].rearrange("p (k f) -> p k f", f=F), ACT.Copy
                                         ).then_inc(sem("part1" + tag), 1)

        def dve_features(dve, c, tag, ring, dst, scale):
            dve.sem_inc(sem("g_read" + tag), 2)
            dve.wait_ge(sem("y" + tag), J)
            c.up(nc.vector.memset(dst[:, :, 3 * F], 1.0))
            with looped(dve, J // 2, (c, 6)) as g2:
                for u in range(2):
                    t0 = g2 * 8 + u * 4
                    dve.wait_ge(sem("g" + tag), g2 * 2 + u + 1)
                    for k in range(4):
                        o, i = ring[:, u, k * F:(k + 1) * F], ps[:, 2 + u, k * F:(k + 1) * F]
                        if scale is None:
                            ins = nc.vector.tensor_copy(o, i)
                        else:
                            ins = nc.vector.tensor_scalar(o, i, col(scale, t0 + k), None, ALU.mult)
                    ins.then_inc(sem("g_read" + tag), 1)
                    r = ring[:, u].rearrange("p (k f) -> p k f", f=F)
                    d = [dst[:, bass.ds(t0, 4), s * F:(s + 1) * F] for s in range(3)]
                    dve.wait_ge(sem("part1" + tag), g2 * 2 + u + 1)
                    c.up(nc.vector.tensor_tensor(r, r, d[0], ALU.subtract))
                    c.wait(dve)
                    c.up(nc.vector.tensor_copy(d[1], r))
                    c.wait(dve)
                    c.up(nc.vector.tensor_tensor(d[2], r, d[1], ALU.subtract))
            c.wait(dve)
            nc.vector.memset(zero_col, 0.0).then_inc(sem("split" + tag), 1)

        def pe_aggregate(pe, i, u, tag, src, width, credit_wait):
            pe.wait_ge(sem("agg" + tag + "_used"), credit_wait)
            for t in range(T):
                ins = nc.tensor.matmul(ps[:, u, 0:width], adj8[:, t, i * P:(i + 1) * P], src[:, t, 0:width],
                                       start=(t == 0), stop=(t == T - 1))
            ins.then_inc(sem("agg" + tag), 1)

        @block.gpsimd
        def _(pool):
            nc.gpsimd.memset(ident[:], 0.0).then_inc(sem("id0"), 1)
            nc.gpsimd.memset(ones[:], 1.0).then_inc(sem("id0"), 1)
            nc.gpsimd.iota(grid[:], [[1, GRID]], base=0, channel_multiplier=0,
                           allow_small_or_imprecise_dtypes=True).then_inc(sem("id0"), 1)
            pool.wait_ge(sem("id0"), 3)
            nc.gpsimd.affine_select(out=ident[:], in_=ident[:], compare_op=ALU.not_equal, fill=1.0, base=0,
                                    pattern=[[-1, P]], channel_multiplier=1).then_inc(sem("ident"), 1)
            with pool.Fori(0, T // 2) as b:
                for u in range(2):
                    pool.wait_ge(sem("v"), b * 2 + u + 1)
                    pool.dma_start(table[bass.ds((b * 2 + u) * P, P), :], vring[:, u, :]
                                   ).then_inc(sem(f"v_stored{u}"), 16)
            pool.wait_ge(sem("norm_bc"), J)
            pool.wait_ge(sem("normp"), 1)
            for j in range(J):
                for t in range(T):
                    pool.wait_ge(sem("pv1"), j * T + t + 1)
                    nc.gpsimd.tensor_scalar(work[:, t % 4, :], norm_bc[:, j * NB:(j + 1) * NB], normp[:, t:t + 1], COS_EPS,
                                            ALU.mult, ALU.add).then_inc(sem("den1"), 1)
            pool.wait_ge(sem("trange"), 1)
            nc.gpsimd.partition_all_reduce(trange[:, 4:8], trange[:, 0:4], P, RMAX).then_inc(sem("trange_all"), 1)

        @block.scalar
        def _(act):
            act_front(act, "0", ht0)
            act_features(act, "0", ring0, gs)
            act.sem_inc(sem("cast"), STAGES)
            with act.Fori(0, QB) as b:
                for q in range(QT):
                    act.wait_ge(sem(f"adj_in{q % STAGES}"), b * (16 * (QT // STAGES)) + 16 * (q // STAGES) + 16)
                    nc.scalar.activation(adj_u8[:, q * TQ:(q + 1) * TQ, bass.ds(b * NQ, NQ)], stage[:, q % STAGES],
                                         ACT.Copy, scale=ONE8).then_inc(sem("cast"), 1)
            act.sem_inc(sem("vt"), 2)
            with act.Fori(0, J // 2) as g2:
                for u in range(2):
                    act.wait_ge(sem("vt_ps"), g2 * 2 + u + 1)
                    nc.scalar.activation(blk(vt, g2 * 2 + u), ps[:, u, :], ACT.Copy).then_inc(sem("vt"), 1)

            act.sem_inc(sem("column"), 2)
            with act.Fori(0, N // 2) as n2:
                for p2 in range(2):
                    act.wait_ge(sem("row_max"), n2 * 2 + p2 + 1)
                    nc.scalar.activation(column[:, p2, :], adj_u8[:, :, bass.ds(n2 * 2 + p2, 1)].rearrange("p t o -> p (t o)"),
                                         ACT.Copy, scale=1.0 / ONE8).then_inc(sem("column"), 1)

            act_front(act, "1", ht)
            act.sem_inc(sem("hp"), 2)
            with act.Fori(0, J // 2) as g2:
                for u in range(2):
                    act.wait_ge(sem("hp_ps"), g2 * 2 + u + 1)
                    nc.scalar.activation(hp[:, bass.ds(g2 * 8 + u * 4, 4), 0:F],
                                         ps[:, 2 + u].rearrange("p (k f) -> p k f", f=F), ACT.Copy
                                         ).then_inc(sem("hp"), 1)
            act.wait_ge(sem("sumsq"), 1)
            nc.scalar.activation(normp, normp, ACT.Sqrt).then_inc(sem("normp"), 1)
            act.sem_inc(sem("sumsq_bc"), 2)
            with act.Fori(0, J // 2) as g2:
                for u in range(2):
                    act.wait_ge(sem("sumsq_bc"), g2 * 2 + u + 1)
                    nc.scalar.activation(work[:, u, :], blk(ht, g2 * 2 + u), ACT.Square).then_inc(sem("sq"), 1)
                    act.wait_ge(sem("sumsq_bc"), g2 * 2 + u + 3)
                    nc.scalar.activation(blk(norm_bc, g2 * 2 + u), ps[:, u, :], ACT.Sqrt).then_inc(sem("norm_bc"), 1)
            nc.scalar.preload_act_table(ACT.Exp)
            act.wait_ge(sem("beta"), 1)
            with act.Fori(0, J) as j:
                with act.Fori(0, T // 4) as tt:
                    for u in range(4):
                        act.wait_ge(sem("cos1"), j * T + tt * 4 + u + 5)
                        nc.scalar.activation(work[:, u, :], work[:, u, :], ACT.Exp, bias=nbeta, scale=beta_col
                                             ).then_inc(sem("exp1"), 1)
            act_front(act, "2", ht)
            act.wait_ge(sem("deg1"), 1)
            nc.scalar.activation(degs, degs, ACT.Sqrt).then_inc(sem("deg_sqrt"), 1)
            nc.scalar.activation(degp, degp, ACT.Sqrt).then_inc(sem("deg_sqrt"), 1)
            act_features(act, "2", work, gs2)
            act_front(act, "3", ht)
            act.sem_inc(sem("cp"), 2)
            with act.Fori(0, T // 4) as g2:
                for u in range(2):
                    t0 = g2 * 4 + u * 2
                    act.wait_ge(sem("cp_ps"), g2 * 2 + u + 1)
                    src = ps[:, 2 + u, 0:2 * (F + 2)].rearrange("p (k f) -> p k f", f=F + 2)
                    dst = cp[:, bass.ds(t0, 2), :, 0:FH]
                    for k in range(2):
                        nc.scalar.activation(cp[:, bass.ds(t0 + k, 1), :, 0:FH].rearrange("p o h f -> p (o h) f"),
                                             src[:, k, 0:F].rearrange("p (h f) -> p h f", h=HEADS), ACT.Copy)
                    nc.scalar.activation(tneigh[:, bass.ds(t0, 2), :], src[:, :, F:F + 2], ACT.Copy
                                         ).then_inc(sem("cp"), 1)
            nc.scalar.preload_act_table(ACT.Exp)
            with act.Fori(0, J) as j:
                for h in range(HEADS):
                    act.wait_ge(sem("s_ps"), j * HEADS + h + 1)
                    if h == 0:
                        act.wait_ge(sem("x3b"), j + 1)
                    nc.scalar.activation(rows[:, 0, h, :], ps[:, 1 + h, :], ACT.Copy).then_inc(sem("s_row"), 1)
                for h in range(HEADS):
                    act.wait_ge(sem("zmax"), j * HEADS + h + 1)
                    nc.scalar.activation(rows[:, 1, h, :], rows[:, 2, h, :], ACT.Exp).then_inc(sem("ezmax"), 1)
                act.wait_ge(sem("m_row"), j + 1)
                with act.Fori(0, T // 2) as tt:
                    for u in range(2):
                        g = j * T + tt * 2 + u
                        act.wait_ge(sem("pv3"), g + 1)
                        for h in range(HEADS):
                            nc.scalar.activation(work[:, 2 * u + h, :], rows[:, 0, h, :], ACT.Exp,
                                                 bias=tile(tneigh, tt * 2 + u)[:, h:h + 1]).then_inc(sem("ez3"), 1)
                    for u in range(2):
                        for h in range(HEADS):
                            act.wait_ge(sem("score3"), j * (T * 2) + tt * 4 + u * 2 + h + 1)
                            nc.scalar.activation(work[:, 2 * u + h, :], work[:, 2 * u + h, :], ACT.Exp
                                                 ).then_inc(sem("exp3"), 1)

        @block.tensor
        def _(pe):
            pe.wait_ge(sem("ident"), 1)
            pe_front(pe, "0", ring0)
            pe.wait_ge(sem("w_in"), 16 * 6)
            pe_features(pe, "0", ht0, w0s[:])
            pe.wait_ge(sem("split0"), 1)
            for b in range(QB):
                pe.wait_ge(sem("cast"), b * QT + STAGES + QT)
                for u in range(2):
                    pe_aggregate(pe, b * 2 + u, u, "0", gs, 3 * F + 1, b * 2 + u + 1)
            pe.wait_ge(sem("tp_in"), 16)
            pe.wait_ge(sem("agg0_used"), 2 + T)
            for g2 in range(J // 2):
                for u in range(2):
                    pe.wait_ge(sem("vt"), g2 * 2 + u + 1)
                    for k in range(4):
                        ins = nc.tensor.transpose(ps[:, u, k * P:(k + 1) * P], tile(tp, g2 * 8 + u * 4 + k), ident[:])
                    ins.then_inc(sem("vt_ps"), 1)
            pe.wait_ge(sem("vt"), 2 + J)
            with pe.Fori(0, N // 2) as n2:
              for p2 in range(2):
                n = n2 * 2 + p2
                for half in range(2):
                    if half == 0:
                        pe.wait_ge(sem("column"), n + 3)
                    pe.wait_ge(sem("mask_used"), n * 2 + half + 1)
                    for t in range(T // 2):
                        tt = half * (T // 2) + t
                        ins = nc.tensor.matmul(ps[:, 4 * half + t // 4, (t % 4) * P:(t % 4 + 1) * P],
                                               column[:, p2, tt:tt + 1].to_broadcast([P, P]), ident_bf[:],
                                               start=True, stop=True)
                    ins.then_inc(sem("mask"), 1)
            pe.wait_ge(sem("pooled"), 1)
            for g2 in range(J // 2):
                for u in range(2):
                    pe.wait_ge(sem("x0"), g2 * 2 + u + 1)
                    for k in range(4):
                        ins = nc.tensor.transpose(ps[:, u, k * P:(k + 1) * P], blk(dt_, g2 * 8 + u * 4 + k, P), ident[:])
                    ins.then_inc(sem("pooled_ps"), 1)

            pe_front(pe, "1", work)
            pe.wait_ge(sem("ht1"), 2 + J)
            for g2 in range(J // 2):
                for u in range(2):
                    pe.wait_ge(sem("hp"), g2 * 2 + u + 1)
                    for k in range(4):
                        ins = nc.tensor.transpose(ps[:, 2 + u, k * F:(k + 1) * F], spread(ht, g2 * 8 + u * 4 + k), ident[:])
                    ins.then_inc(sem("hp_ps"), 1)
            with pe.Fori(0, J // 2) as g2:
                for u in range(2):
                    pe.wait_ge(sem("sq"), g2 * 2 + u + 1)
                    nc.tensor.matmul(ps[:, u, :], ones[:], work[:, u, :], start=True, stop=True
                                     ).then_inc(sem("sumsq_bc"), 1)
            pe.wait_ge(sem("norm_bc"), J)
            pe.wait_ge(sem("hp"), 2 + J)
            pe.sem_inc(sem("pv1"), 4)

            def dots(j, t, u, g):
                pe.wait_ge(sem("cos1"), g + 1)
                nc.tensor.matmul(ps[:, u, :], spread(ht, t), blk(ht, j), start=True, stop=True).then_inc(sem("dot1"), 1)

            def weigh(t, u, g, first, last):
                pe.wait_ge(sem("prob1"), g + 1)
                for s in range(4):
                    ins = nc.tensor.matmul(ps[:, 4 + s, 0:F + 1], work[:, u, s * P:(s + 1) * P], tile(hp, t)[:, 0:F + 1],
                                           start=first, stop=last)
                ins.then_inc(sem("pv1"), 1)

            def block1(j, last_block):
                pe.wait_ge(sem("x1b"), j + 1)
                for t in range(T):
                    weigh(t, t % 4, j * T + t, t == 0, t == T - 1)
                    if t + 4 < T:
                        dots(j, t + 4, t % 4, j * T + t + 4)
                    elif not last_block:
                        dots(j + 1, t + 4 - T, t % 4, j * T + t + 4)

            for u in range(4):
                dots(0, u, u, u)
            with pe.Fori(0, J - 1) as j:
                block1(j, False)
            block1(J - 1, True)

            pe_front(pe, "2", work)
            pe_features(pe, "2", ht, w2s[:])
            pe.wait_ge(sem("split2"), 1)
            for b in range(T // 2):
                for u in range(2):
                    pe_aggregate(pe, b * 2 + u, u, "2", gs2, 3 * F, b * 2 + u + 1)

            pe_front(pe, "3", work)
            pe.wait_ge(sem("ht3"), 2 + J)
            pe.wait_ge(sem("att"), 1)
            for g2 in range(T // 4):
                for u in range(2):
                    pe.wait_ge(sem("cp"), g2 * 2 + u + 1)
                    for k in range(2):
                        ins = nc.tensor.matmul(ps[:, 2 + u, k * (F + 2):(k + 1) * (F + 2)],
                                               spread(ht, g2 * 4 + u * 2 + k), k3s[:], start=True, stop=True)
                    ins.then_inc(sem("cp_ps"), 1)
            pe.wait_ge(sem("cp"), 2 + T // 2)
            pe.wait_ge(sem("ind"), 1)
            for j in range(J):
                if j >= 2:
                    pe.wait_ge(sem("over_raw"), j - 1)
                for t in range(T):
                    ins = nc.tensor.matmul(ps[:, j % 2, :], ind[:, t, :], adj8[:, t, j * NB:(j + 1) * NB],
                                           start=(t == 0), stop=(t == T - 1))
                ins.then_inc(sem("cnt"), 1)
            pe.wait_ge(sem("over"), 1)
            pe.sem_inc(sem("pv3"), 2)
            with pe.Fori(0, J) as j:
                pe.wait_ge(sem("x3b"), j + 1)
                for h in range(HEADS):
                    nc.tensor.matmul(ps[:, 1 + h, :], s_w[h], blk(ht, j), start=True, stop=True).then_inc(sem("s_ps"), 1)
                pe.wait_ge(sem("over_j"), j + 1)
                for h in range(HEADS):
                    nc.tensor.matmul(ps[:, 3 * (1 - h), :], head_ones[:, h, :], over_j, start=True, stop=True
                                     ).then_inc(sem("steps"), 1)

                def weigh3(tt, first, last):
                    for u in range(2):
                        pe.wait_ge(sem("prob3"), j * (T * 2) + tt * 4 + u * 2 + 2)
                        for s in range(4):
                            for h in range(HEADS):
                                ins = nc.tensor.matmul(ps[:, 4 + s, h * (FH + 1):(h + 1) * (FH + 1)],
                                                       work[:, 2 * u + h, s * P:(s + 1) * P],
                                                       cp[:, bass.ds(tt * 2 + u, 1), h, :].rearrange("p o f -> p (o f)"),
                                                       start=(first and u == 0 and h == 0),
                                                       stop=(last and u == 1 and h == 1), skip_group_check=True)
                        ins.then_inc(sem("pv3"), 1)

                weigh3(0, True, False)
                with pe.Fori(1, T // 2 - 1) as tt:
                    weigh3(tt, False, False)
                weigh3(T // 2 - 1, False, True)

        @block.vector
        def _(dve):
            c = Tally(sem("dve_chain"))
            c.up(nc.vector.memset(zero_col, 0.0))
            dve.wait_ge(sem("ident"), 1)
            c.up(nc.vector.tensor_copy(ident_bf[:], ident[:]))
            dve.wait_ge(sem("x0_in"), 16)
            dve_front(dve, c, "0", x0, ring0)
            dve_features(dve, c, "0", ring0, gs, None)
            dve.wait_ge(sem("w_in"), 16 * 6)
            dve.sem_inc(sem("agg0_used"), 2)

            def activate0(b, stored):
                for u in range(2):
                    i = b * 2 + u
                    dve.wait_ge(sem("agg0"), i + 1)
                    if stored is not None:
                        dve.wait_ge(sem(f"v_stored{u}"), stored)
                    c.up(nc.vector.tensor_reduce(vring[:, u, :], ps[:, u, 0:3 * F].rearrange("p (s f) -> p f s", s=3),
                                                 AX_X, ALU.add))
                    nc.vector.tensor_copy(col(degs, i), ps[:, u, 3 * F:3 * F + 1]).then_inc(sem("agg0_used"), 1)
                    c.wait(dve)
                    c.up(nc.vector.tensor_tensor(vring[:, u, :], vring[:, u, :], b0s[:], ALU.add))
                    c.wait(dve)
                    nc.vector.tensor_scalar(vring[:, u, :], vring[:, u, :], 0.0, None, ALU.max).then_inc(sem("v"), 1)

            activate0(0, None)
            with looped(dve, T // 2 - 1, (c, 4)) as b:
                activate0(b + 1, b * 16 + 16)
            dve.wait_ge(sem("agg0_used"), 2 + T)
            c.up(nc.vector.tensor_scalar(none, degs, 0.0, F32_MIN, ALU.is_equal, ALU.mult))
            dve.wait_ge(sem("vt"), 2 + J)
            dve.sem_inc(sem("mask_used"), 2)
            dve.sem_inc(sem("row_max"), 2)
            with dve.Fori(0, N) as n:
                for half in range(2):
                    if half:
                        dve.wait_ge(sem("mask_used"), n * 2 + half + 2)
                    wait_reg(dve, sem("mask"), n * 2 + half + 1)
                    nc.vector.tensor_tensor_reduce(junk, vt[:, half * HB:(half + 1) * HB],
                                                   ps[:, 4 * half:4 * half + 4, :].rearrange("p b n -> p (b n)"), 1.0,
                                                   rowmax if half else 0.0, ALU.mult, ALU.max,
                                                   rowmax2 if half else rowmax).then_inc(sem("mask_used"), 1)
                dve.wait_ge(sem("mask_used"), n * 2 + 4)
                nc.vector.tensor_copy(col(dt_, n), rowmax2).then_inc(sem("row_max"), 1)
            dve.wait_ge(sem("row_max"), 2 + N)
            nc.vector.memset(zero_col, 0.0).then_inc(sem("pooled"), 1)
            dve.wait_ge(sem("xr_in"), 16)
            dve.sem_inc(sem("x0"), 2)
            with dve.Fori(0, J // 2) as g2:
                for u in range(2):
                    dve.wait_ge(sem("pooled_ps"), g2 * 2 + u + 1)
                    for k in range(4):
                        i = g2 * 8 + u * 4 + k
                        ins = nc.vector.scalar_tensor_tensor(tile(xr, i), ps[:, u, k * P:(k + 1) * P], col(none, i),
                                                             tile(xr, i), ALU.add, ALU.add)
                    ins.then_inc(sem("x0"), 1)
            dve.wait_ge(sem("x0"), 2 + J)

            dve_front(dve, c, "1", xr, work)
            dve.wait_ge(sem("hp"), 2 + J)
            c.up(nc.vector.memset(hp[:, :, F], 1.0))
            for t in range(T):
                c.wait(dve)
                c.up(nc.vector.tensor_tensor_reduce(work[:, 3, 0:F], hp[:, t, 0:F], hp[:, t, 0:F], 1.0, 0.0,
                                                    ALU.mult, ALU.add, normp[:, t:t + 1]))
            c.wait(dve)
            nc.vector.memset(zero_col, 0.0).then_inc(sem("sumsq"), 1)
            c.up(nc.vector.tensor_scalar(nbeta, beta_col, -1.0, None, ALU.mult))
            c.wait(dve)
            nc.vector.tensor_tensor(nbeta, nbeta, beta_col, ALU.min).then_inc(sem("beta"), 1)
            dve.sem_inc(sem("cos1"), 4)
            dve.sem_inc(sem("x1b"), 1)
            with looped(dve, J, (c, T + 1)) as j:
                with looped(dve, T // 4, (c, 4)) as tt:
                    def cosines(u):
                        g = j * T + tt * 4 + u
                        w = work[:, u, :]
                        dve.wait_ge(sem("den1"), g + 1)
                        c.up(nc.vector.reciprocal(w, w))
                        dve.wait_ge(sem("dot1"), g + 1)
                        c.wait(dve)
                        nc.vector.tensor_tensor(w, w, ps[:, u, :], ALU.mult).then_inc(sem("cos1"), 1)

                    def masked(u):
                        w = work[:, u, :]
                        dve.wait_ge(sem("exp1"), j * T + tt * 4 + u + 1)
                        nc.vector.tensor_tensor(w, w, adj_u8[:, bass.ds(tt * 4 + u, 1), bass.ds(j * NB, NB)].rearrange(
                            "p o n -> p (o n)"), ALU.mult).then_inc(sem("prob1"), 1)

                    cosines(0)
                    cosines(1)
                    masked(0)
                    cosines(2)
                    masked(1)
                    cosines(3)
                    masked(2)
                    masked(3)
                dve.wait_ge(sem("pv1"), j * T + T + 4)
                c.up(nc.vector.reciprocal(rinv, ps[:, 4:8, F]))
                c.wait(dve)
                for s in range(4):
                    ins = nc.vector.scalar_tensor_tensor(tile(xr, j * 4 + s), ps[:, 4 + s, 0:F], rinv[:, s:s + 1],
                                                         tile(xr, j * 4 + s), ALU.mult, ALU.add)
                ins.then_inc(sem("x1b"), 1)
            dve.wait_ge(sem("x1b"), 1 + J)

            dve.wait_ge(sem("deg_in"), 16)
            for d in (degs, degp):
                c.up(nc.vector.tensor_scalar(d, d, 1.0, 1e-12, ALU.add, ALU.max))
            c.wait(dve)
            nc.vector.memset(zero_col, 0.0).then_inc(sem("deg1"), 1)
            dve_front(dve, c, "2", xr, work)
            dve.wait_ge(sem("deg_sqrt"), 2)
            for d in (degs, degp):
                c.up(nc.vector.reciprocal(d, d))
            c.wait(dve)
            for t in range(T):
                d = spread(adj8[:, t, :], t)
                c.up(nc.vector.tensor_tensor(d, d, ident[:], ALU.add, saturate=False))
            dve_features(dve, c, "2", work, gs2, degp)
            dve.sem_inc(sem("agg2_used"), 2)
            with looped(dve, T // 2, (c, 4)) as b:
                for u in range(2):
                    i = b * 2 + u
                    a = work[:, u, 0:F]
                    dve.wait_ge(sem("agg2"), i + 1)
                    nc.vector.tensor_reduce(a, ps[:, u, 0:3 * F].rearrange("p (s f) -> p f s", s=3), AX_X, ALU.add
                                            ).then_inc(sem("agg2_used"), 1)
                    dve.wait_ge(sem("agg2_used"), i + 3)
                    c.up(nc.vector.scalar_tensor_tensor(a, a, col(degs, i), b2s[:], ALU.mult, ALU.add))
                    c.wait(dve)
                    c.up(nc.vector.scalar_tensor_tensor(tile(xr, i), a, 0.0, tile(xr, i), ALU.max, ALU.add))
            c.wait(dve)
            nc.vector.memset(zero_col, 0.0).then_inc(sem("x2"), 1)
            for t in range(T):
                d = spread(adj8[:, t, :], t)
                c.up(nc.vector.tensor_tensor(d, d, ident[:], ALU.subtract, saturate=False))

            dve.wait_ge(sem("att_in"), 16)
            for h in range(HEADS):
                for which, dst in ((0, s_col[:, h:h + 1]), (1, k3s[:, F + h:F + h + 1])):
                    c.wait(dve)
                    c.up(nc.vector.tensor_tensor_reduce(work[:, 1, 0:FH], k3s[:, h * FH:(h + 1) * FH],
                                                        work[:, 0, h * F + which * FH:h * F + (which + 1) * FH],
                                                        1.0, 0.0, ALU.mult, ALU.add, dst))
            c.wait(dve)
            for h in range(HEADS):
                c.up(nc.vector.tensor_scalar(s_w[h], ones[:], s_col[:, h:h + 1], None, ALU.mult))
            for h in range(HEADS):
                c.up(nc.vector.memset(head_ones[:, h, :], 0.0))
                c.wait(dve)
                c.up(nc.vector.memset(head_ones[h * GRID:(h + 1) * GRID, h, :], 1.0))
            c.wait(dve)
            nc.vector.memset(zero_col, 0.0).then_inc(sem("att"), 1)
            dve_front(dve, c, "3", xr, work)
            dve.wait_ge(sem("cp"), 2 + T // 2)
            c.up(nc.vector.memset(cp[:, :, :, FH], 1.0))
            tv = tneigh.rearrange("p t h -> p h t")
            c.up(nc.vector.tensor_reduce(trange[:, 0:2], tv, AX_X, ALU.max))
            c.up(nc.vector.tensor_reduce(trange[:, 2:4], tv, AX_X, ALU.min))
            c.wait(dve)
            nc.vector.tensor_scalar(trange[:, 2:4], trange[:, 2:4], -1.0, None, ALU.mult).then_inc(sem("trange"), 1)
            dve.wait_ge(sem("trange_all"), 1)
            c.up(nc.vector.tensor_tensor(tstep, trange[:, 4:6], trange[:, 6:8], ALU.add))
            c.up(nc.vector.tensor_scalar(tmin, trange[:, 6:8], -1.0, None, ALU.mult))
            c.wait(dve)
            c.up(nc.vector.tensor_scalar(tstep, tstep, 1.0 / GRID, None, ALU.mult))
            c.wait(dve)
            for h in range(HEADS):
                c.up(nc.vector.tensor_scalar(theta[:, h, :], grid[:], tstep[:, h:h + 1], tmin[:, h:h + 1],
                                             ALU.mult, ALU.add))
            c.wait(dve)
            for t in range(T):
                for h in range(HEADS):
                    c.up(nc.vector.tensor_scalar(ind[:, t, :][:, h * GRID:(h + 1) * GRID], theta[:, h, :],
                                                 tile(tneigh, t)[:, h:h + 1], None, ALU.is_le, saturate=False))
            c.wait(dve)
            nc.vector.memset(zero_col, 0.0).then_inc(sem("ind"), 1)
            for j in range(J):
                dve.wait_ge(sem("cnt"), j + 1)
                nc.vector.tensor_scalar(over_raw[:, j * NB:(j + 1) * NB], ps[:, j % 2, :], 0.5, None, ALU.is_gt).then_inc(sem("over_raw"), 1)
            dve.wait_ge(sem("over_raw"), J)
            nc.vector.tensor_copy(view(49408, 4096, F32), view(53504, 4096, F32)).then_inc(sem("over"), 1)
            dve.wait_ge(sem("over"), 1)
            dve.sem_inc(sem("x3b"), 1)
            with looped(dve, J, (c, 8 + 2 * T + 1)) as j:
                nc.vector.tensor_copy(over_j, blk(over, j)).then_inc(sem("over_j"), 1)
                for h in range(HEADS):
                    dve.wait_ge(sem("steps"), j * HEADS + h + 1)
                    c.up(nc.vector.tensor_scalar(rows[:, 2, h, :], ps[:, 3 * (1 - h), :], tstep[:, h:h + 1],
                                                 tmin[:, h:h + 1], ALU.mult, ALU.add))
                    c.wait(dve)
                    dve.wait_ge(sem("s_row"), j * HEADS + h + 1)
                    nc.vector.tensor_tensor(rows[:, 2, h, :], rows[:, 2, h, :], rows[:, 0, h, :], ALU.add
                                            ).then_inc(sem("zmax"), 1)
                for h in range(HEADS):
                    s, a, m = (rows[:, r, h, :] for r in range(3))
                    dve.wait_ge(sem("ezmax"), j * HEADS + h + 1)
                    c.up(nc.vector.tensor_scalar(a, a, 1.0, -1.0, ALU.min, ALU.add))
                    c.wait(dve)
                    c.up(nc.vector.tensor_tensor(m, m, a, ALU.max))
                    c.wait(dve)
                    c.up(nc.vector.tensor_tensor(a, s, m, ALU.subtract))
                for h in range(HEADS):
                    ins = nc.vector.tensor_scalar(rows[:, 2, h, :], rows[:, 2, h, :], 1.0, None, ALU.add)
                ins.then_inc(sem("m_row"), 1)
                wait_reg(dve, sem("m_row"), j + 1)
                with looped(dve, T // 2, (c, 4)) as tt:
                    for u in range(2):
                        for h in range(HEADS):
                            w = work[:, 2 * u + h, :]
                            dve.wait_ge(sem("ez3"), j * (T * 2) + tt * 4 + u * 2 + h + 1)
                            c.up(nc.vector.scalar_tensor_tensor(w, w, 1.0, rows[:, 2, h, :], ALU.min, ALU.subtract))
                            c.wait(dve)
                            nc.vector.scalar_tensor_tensor(w, rows[:, 1, h, :], tile(tneigh, tt * 2 + u)[:, h:h + 1], w,
                                                           ALU.add, ALU.max).then_inc(sem("score3"), 1)
                    for u in range(2):
                        for h in range(HEADS):
                            w = work[:, 2 * u + h, :]
                            dve.wait_ge(sem("exp3"), j * (T * 2) + tt * 4 + u * 2 + h + 1)
                            nc.vector.scalar_tensor_tensor(w, w, 2.0, adj_u8[:, bass.ds(tt * 2 + u, 1),
                                                           bass.ds(j * NB, NB)].rearrange("p o n -> p (o n)"),
                                                           ALU.min, ALU.mult).then_inc(sem("prob3"), 1)
                dve.wait_ge(sem("pv3"), j * T + T + 2)
                for h in range(HEADS):
                    o = h * (FH + 1)
                    ins = nc.vector.reciprocal(rinv[:, 0:4] if h == 0 else rinv2, ps[:, 4:8, o + FH])
                c.up(ins)
                c.wait(dve)
                for s in range(4):
                    for h in range(HEADS):
                        o = h * (FH + 1)
                        xt = tile(xr, j * 4 + s)[:, h * FH:(h + 1) * FH]
                        r = (rinv if h == 0 else rinv2)[:, s:s + 1]
                        ins = nc.vector.scalar_tensor_tensor(xt, ps[:, 4 + s, o:o + FH], r, xt, ALU.mult, ALU.add)
                ins.then_inc(sem("x3b"), 1)
            dve.wait_ge(sem("x3b"), 1 + J)
            nc.vector.memset(zero_col, 0.0).then_inc(sem("x3"), 1)


def kernel(**inputs):
    import numpy as _np
    import concourse.bacc as _bacc
    from concourse import mybir as _mybir
    from concourse.bass_utils import run_bass_kernel_spmd as _run

    nc = _bacc.Bacc("TRN2", target_bir_lowering=False, num_devices=1)
    arrays = {
        "x_in": inputs["x"],
        "adj_t": _np.asarray(inputs["adj"]).T,
        "w0": inputs["L0_gnn_weight"],
        "b0": inputs["L0_gnn_bias"],
        "beta": inputs["L1_gnn_beta"],
        "w2t": _np.asarray(inputs["L2_gnn_W"]).T,
        "b2": inputs["L2_gnn_b"],
        "k3": inputs["L3_gnn_kernels"],
        "att": inputs["L3_gnn_att_kernels"],
    }
    arrays = {n: _np.ascontiguousarray(a) for n, a in arrays.items()}
    args = [nc.dram_tensor(n, a.shape, _mybir.dt.from_np(a.dtype), kind="ExternalInput").ap()
            for n, a in arrays.items()]
    out = nc.dram_tensor("out_0", (4096, 128), _mybir.dt.float32, kind="ExternalOutput").ap()
    build(nc, *args, out)
    r = _run(nc, [arrays], core_ids=[0])
    return r.results[0]["out_0"]
```

```python
from contextlib import ExitStack

import concourse.bass as bass
from concourse import mybir

P = 128
F = 128
N = 4096
T = N // P
HEADS = 2
FH = F // HEADS
NB = 512
J = N // NB
GRID = P // HEADS
CHUNK = 4
CHUNKS = T // CHUNK
KEEP = 32
KEY0 = 134 * P
GATHERS = 4
LN_EPS = 1e-5
COS_EPS = 1e-7
TINY = 1e-18
F32_MIN = -3.4028234663852886e38

ALU = mybir.AluOpType
ACT = mybir.ActivationFunctionType
F32 = mybir.dt.float32
BF16 = mybir.dt.bfloat16
FP8 = mybir.dt.float8e4
I32 = mybir.dt.int32
U32 = mybir.dt.uint32
U8 = mybir.dt.uint8
AX_X = mybir.AxisListType.X
RMAX = bass.bass_isa.ReduceOp.max
RADD = bass.bass_isa.ReduceOp.add



class Tally:

    def __init__(self, sem):
        self.sem, self.n = sem, 0

    def up(self, ins):
        ins.then_inc(self.sem, 1)
        self.n = self.n + 1
        return ins

    def wait(self, eng):
        eng.wait_ge(self.sem, self.n)


class looped:

    def __init__(self, eng, count, *tallies):
        self.eng, self.count, self.tallies = eng, count, tallies

    def __enter__(self):
        self.cm = self.eng.Fori(0, self.count)
        i = self.cm.__enter__()
        self.base = [t.n for t, _ in self.tallies]
        for (t, per), b in zip(self.tallies, self.base):
            t.n = i * per + b
        return i

    def __exit__(self, *exc):
        r = self.cm.__exit__(*exc)
        for (t, per), b in zip(self.tallies, self.base):
            t.n = b + self.count * per
        return r


def build(nc, x, adj_t, w0, b0, beta, w2t, b2, k3, att, out):
    with ExitStack() as ctx:
        def sb(name, shape, dt):
            return ctx.enter_context(nc.sbuf_tensor(name, shape, dt))

        sems = {}

        def sem(name):
            if name not in sems:
                sems[name] = ctx.enter_context(nc.semaphore(name))
            return sems[name]

        list_dram = nc.dram_tensor("dense_rows", (2 * N, 1), I32).ap()
        table = nc.dram_tensor("v_table", (N + 1, F), F32).ap()
        deg_dram = nc.dram_tensor("deg_rows", (N,), F32).ap()

        adj8 = sb("adj8", [P, T, N], FP8)
        ONE8 = 56.0
        adj_u8 = adj8[:].bitcast(U8)
        arena = sb("arena", [P, 73984 // 4], F32)

        def view(at, nbytes, dt):
            v = arena[:, at // 4:(at + nbytes) // 4]
            return v if dt == F32 else v.bitcast(dt)

        SPLIT_W = 3 * F + 2
        x0 = view(0, 16384, F32).rearrange("p (i f) -> p i f", f=F)
        ht0 = view(24704, 16384, F32)
        gs = view(0, 24704, BF16).rearrange("p (t c) -> p t c", c=SPLIT_W)
        ring0 = view(41088, 8192, F32).rearrange("p (b c) -> p b c", c=NB)
        STAGES, TQ, NQ = 4, 4, 256
        stage = view(49408, 16384, F32).rearrange("p (s t n) -> p s t n", s=STAGES, n=NQ)
        key_diag = view(41088, 8192, BF16).rearrange("p (t k) -> p t k", k=P)
        slots = view(65792, 512, F32).rearrange("p (b k) -> p b k", b=2)
        keys = view(25728, 4096, F32).rearrange("p (i k) -> p i k", k=KEEP)
        tmp = [view(b, 4096, I32) for b in (0, 4096)]
        tri = view(8192, 512, F32)
        flag = view(8704, 128, F32)
        cnt = view(8832, 128, F32)
        seen = view(8960, 128, F32)
        pos = view(9088, 128, I32)
        posf = view(9216, 128, F32)
        ids = view(9344, 128, I32)
        scan = view(9472, 512, F32).rearrange("p (b w i) -> p b w i", b=2, w=2)
        tile_max = view(9984, 256, F32).rearrange("p (w i) -> p w i", w=2)
        rows_list = view(0, 16384, I32)[0:1, :]
        pooled = view(16384, 16384, F32).rearrange("p (i f) -> p i f", f=F)
        index = view(65792, 4096, I32).rearrange("p (i k) -> p i k", k=KEEP)
        gathered = view(69888, 2048, F32).rearrange("p (s f) -> p s f", f=F)
        vring = view(24704, 1024, F32).rearrange("p (b f) -> p b f", b=2)
        xr = view(0, 16384, F32).rearrange("p (i f) -> p i f", f=F)
        ht = view(16384, 16384, F32)
        tp = view(32768, 16384, F32).rearrange("p (t f) -> p t f", f=F)
        dt_ = view(32768, 16384, F32)
        hp = view(32768, 16640, F32).rearrange("p (t c) -> p t c", c=130)
        gs2 = view(32768, 24704, BF16).rearrange("p (t c) -> p t c", c=SPLIT_W)
        vt = view(49408, 16384, F32)
        inv_bc = view(49408, 16384, F32)
        work = view(65792, 8192, F32).rearrange("p (b c) -> p b c", c=NB)
        junk = view(71936, 2048, U8)
        ind = view(49408, 4096, FP8).rearrange("p (t k) -> p t k", k=P)
        rows = view(53504, 12288, F32).rearrange("p (r h n) -> p r h n", r=3, n=NB)

        ident = sb("ident", [P, P], F32)
        ident_bf = sb("ident_bf", [P, P], BF16)
        ones = sb("ones", [P, P], F32)
        w0s = sb("w0s", [P, F], F32)
        w2s = sb("w2s", [P, F], F32)
        b0s = sb("b0s", [P, F], F32)
        b2s = sb("b2s", [P, F], F32)
        k3s = sb("k3s", [P, F + 2], F32)
        small = sb("small", [P, 512], F32)
        stats = small[:, 0:192].rearrange("p (i c) -> p i c", c=6)
        mv = small[:, 192:256].rearrange("p (i c) -> p i c", c=2)
        rstd = small[:, 256:288]
        degs = small[:, 288:320]
        degp = small[:, 320:352]
        none = small[:, 352:384]
        normp = small[:, 384:416]
        neg_eps_inv = normp
        misc = small[:, 416:512]
        eps_col = misc[:, 0:1]
        beta_col = misc[:, 1:2]
        nbeta = misc[:, 2:3]
        rowmax = misc[:, 3:4]
        rinv = misc[:, 4:8]
        zero_col = misc[:, 8:9]
        rowmax2 = misc[:, 27:28]
        trange = misc[:, 9:17]
        tstep = misc[:, 17:19]
        tmin = misc[:, 19:21]
        rinv2 = misc[:, 21:25]
        s_col = misc[:, 25:27]
        tneigh = sb("tneigh", [P, T * HEADS], F32)[:].rearrange("p (t h) -> p t h", h=HEADS)
        control = sb("control", [P, 4, T], I32)
        index_now = sb("index_now", [P, GATHERS], I32)[:]
        best = view(66304, 128, F32)
        key_col = misc[:, 28:29]
        column = view(49152, 64, BF16)
        over_j = small[:, 0:256].bitcast(BF16)
        grid = sb("grid", [P, GRID], F32)
        over_raw = view(53504, 4096, U8)
        over = view(49408, 4096, U8)
        s_w = [w0s[:], w2s[:]]
        head_ones = b0s[:].bitcast(BF16).rearrange("p (h m) -> p h m", h=HEADS)
        theta = b2s[:].rearrange("p (h k) -> p h k", h=HEADS)
        cp = view(32768, 16640, F32).rearrange("p (t h c) -> p t h c", h=HEADS, c=FH + 1)

        ps = ctx.enter_context(nc.psum_tensor("ps", [P, 8, NB], F32))

        x_rows = x.rearrange("(i q) f -> q i f", q=P)
        out_rows = out.rearrange("(i q) f -> q i f", q=P)
        adj_spread = adj_t.rearrange("(p t) n -> p t n", p=P)

        def spread(a, t, k=1):
            v = a.rearrange("f (p t) -> f t p", t=T)
            if isinstance(t, int) and k == 1:
                return v[:, t, :]
            return v[:, bass.ds(t, k), :].rearrange("f o p -> f (o p)")

        QB = N // NQ
        QT = T // TQ
        HB = 4 * NB

        block = ctx.enter_context(nc.Block())

        def wait_reg(eng, s, value):
            eng.wait_ge(s, value)
            eng.sem_inc(sem("waits_passed"), 1)

        def tile(a, i):
            return a[:, bass.ds(i, 1), :].rearrange("p o f -> p (o f)")

        def col(a, i):
            return a[:, bass.ds(i, 1)]

        def blk(a, j, w=NB):
            return a[:, bass.ds(j * w, w)]

        @block.sync
        def _(sp):
            sp.dma_start(x0, x_rows).then_inc(sem("x0_in"), 16)
            for dst, src in ((w0s[:], w0), (w2s[:], w2t),
                             (k3s[:, 0:F].rearrange("p (h f) -> p h f", h=HEADS), k3.rearrange("h d f -> d h f")),
                             (b0s[:], b0.partition_broadcast(P)), (b2s[:], b2.partition_broadcast(P)),
                             (beta_col, beta.partition_broadcast(P))):
                sp.dma_start(dst, src).then_inc(sem("w_in"), 16)
            with sp.Fori(0, QB) as b:
                for q in range(QT):
                    sp.wait_ge(sem("cast"), b * QT + q + 1)
                    sp.dma_start(stage[:, q % STAGES], adj_spread[:, q * TQ:(q + 1) * TQ, bass.ds(b * NQ, NQ)]
                                 ).then_inc(sem(f"adj_in{q % STAGES}"), 16)
            sp.wait_ge(sem("agg0_used"), 2 + T)
            with nc.allow_non_contiguous_dma(reason="one word per node, once"):
                sp.dma_start(deg_dram.rearrange("(i q) -> q i", q=P), degs).then_inc(sem("deg_out"), 16)
            sp.wait_ge(sem("deg_out"), 16)
            sp.dma_start(degp, deg_dram.rearrange("(p t) -> p t", p=P)).then_inc(sem("deg_in"), 16)
            for u in range(2):
                sp.wait_ge(sem(f"v_stored{u}"), 16 * (T // 2))
            sp.wait_ge(sem("key_ps"), CHUNKS * T)
            sp.dma_start(tp, table[0:N].rearrange("(p t) f -> p t f", p=P)).then_inc(sem("tp_in"), 16)
            sp.wait_ge(sem("row_put"), 16 * T)
            sp.dma_start(rows_list, list_dram[0:N].rearrange("n o -> o n")).then_inc(sem("rows_in"), 16)
            sp.wait_ge(sem("pooled"), 1)
            sp.dma_start(xr, x_rows).then_inc(sem("xr_in"), 16)
            sp.wait_ge(sem("x2"), 1)
            sp.dma_start(work[:, 0, 0:HEADS * F], att.rearrange("h f -> (h f)").partition_broadcast(P)
                         ).then_inc(sem("att_in"), 16)
            sp.wait_ge(sem("x3"), 1)
            sp.dma_start(out_rows, xr).then_inc(sem("out_stored"), 16)
            sp.wait_ge(sem("out_stored"), 16)

        def dve_front(dve, c, tag, src, ring):
            c.wait(dve)
            for i in range(T):
                c.up(nc.vector.bn_stats(stats[:, i, :], src[:, i, :]))
            c.wait(dve)
            for i in range(T):
                c.up(nc.vector.bn_aggr(mv[:, i, :], stats[:, i, :]))
            c.wait(dve)
            nc.vector.memset(eps_col, LN_EPS).then_inc(sem("var" + tag), 1)
            dve.wait_ge(sem("std" + tag), 1)
            c.up(nc.vector.reciprocal(rstd, rstd))
            c.wait(dve)
            with dve.Fori(0, J // 2) as g2:
                for u in range(2):
                    dve.wait_ge(sem("yt" + tag), g2 * 2 + u + 1)
                    for k in range(4):
                        i = g2 * 8 + u * 4 + k
                        ins = nc.vector.tensor_scalar(ring[:, u, k * F:(k + 1) * F], tile(src, i),
                                                      tile(mv, i)[:, 0:1], col(rstd, i), ALU.subtract, ALU.mult)
                    ins.then_inc(sem("y" + tag), 1)

        def pe_front(pe, tag, ring):
            pe.sem_inc(sem("yt" + tag), 2)
            with pe.Fori(0, J // 2) as g2:
                for u in range(2):
                    pe.wait_ge(sem("y" + tag), g2 * 2 + u + 1)
                    pe.wait_ge(sem("ht" + tag), g2 * 2 + u + 1)
                    for k in range(4):
                        ins = nc.tensor.transpose(ps[:, u, k * F:(k + 1) * F], ring[:, u, k * F:(k + 1) * F], ident[:])
                    ins.then_inc(sem("yt" + tag), 1)

        def act_front(act, tag, dst):
            act.sem_inc(sem("ht" + tag), 2)
            act.wait_ge(sem("var" + tag), 1)
            nc.scalar.activation(rstd, mv[:, :, 1], ACT.Sqrt, bias=eps_col).then_inc(sem("std" + tag), 1)
            with act.Fori(0, J // 2) as g2:
                for u in range(2):
                    act.wait_ge(sem("yt" + tag), g2 * 2 + u + 3)
                    nc.scalar.activation(blk(dst, g2 * 2 + u), ps[:, u, :], ACT.Relu).then_inc(sem("ht" + tag), 1)

        def pe_features(pe, tag, h, w):
            pe.wait_ge(sem("ht" + tag), 2 + J)
            for g2 in range(J // 2):
                for u in range(2):
                    pe.wait_ge(sem("g_read" + tag), g2 * 2 + u + 1)
                    for k in range(4):
                        ins = nc.tensor.matmul(ps[:, 2 + u, k * F:(k + 1) * F], spread(h, g2 * 8 + u * 4 + k), w,
                                               start=True, stop=True)
                    ins.then_inc(sem("g" + tag), 1)

        def act_features(act, tag, ring, dst):
            with act.Fori(0, J // 2) as g2:
                for u in range(2):
                    act.wait_ge(sem("g_read" + tag), g2 * 2 + u + 3)
                    nc.scalar.activation(dst[:, bass.ds(g2 * 8 + u * 4, 4), 0:F],
                                         ring[:, u].rearrange("p (k f) -> p k f", f=F), ACT.Copy
                                         ).then_inc(sem("part1" + tag), 1)

        def dve_features(dve, c, tag, ring, dst, scale):
            dve.sem_inc(sem("g_read" + tag), 2)
            dve.wait_ge(sem("y" + tag), J)
            c.up(nc.vector.memset(dst[:, :, 3 * F], 1.0))
            with looped(dve, J // 2, (c, 6)) as g2:
                for u in range(2):
                    t0 = g2 * 8 + u * 4
                    dve.wait_ge(sem("g" + tag), g2 * 2 + u + 1)
                    for k in range(4):
                        o, i = ring[:, u, k * F:(k + 1) * F], ps[:, 2 + u, k * F:(k + 1) * F]
                        if scale is None:
                            ins = nc.vector.tensor_copy(o, i)
                        else:
                            ins = nc.vector.tensor_scalar(o, i, col(scale, t0 + k), None, ALU.mult)
                    ins.then_inc(sem("g_read" + tag), 1)
                    r = ring[:, u].rearrange("p (k f) -> p k f", f=F)
                    d = [dst[:, bass.ds(t0, 4), s * F:(s + 1) * F] for s in range(3)]
                    dve.wait_ge(sem("part1" + tag), g2 * 2 + u + 1)
                    c.up(nc.vector.tensor_tensor(r, r, d[0], ALU.subtract))
                    c.wait(dve)
                    c.up(nc.vector.tensor_copy(d[1], r))
                    c.wait(dve)
                    c.up(nc.vector.tensor_tensor(d[2], r, d[1], ALU.subtract))
            c.wait(dve)
            nc.vector.memset(zero_col, 0.0).then_inc(sem("split" + tag), 1)

        def pe_aggregate(pe, i, u, tag, src, width, credit_wait):
            pe.wait_ge(sem("agg" + tag + "_used"), credit_wait)
            for t in range(T):
                ins = nc.tensor.matmul(ps[:, u, 0:width], adj8[:, t, i * P:(i + 1) * P], src[:, t, 0:width],
                                       start=(t == 0), stop=(t == T - 1))
            ins.then_inc(sem("agg" + tag), 1)

        @block.gpsimd
        def _(pool):
            nc.gpsimd.memset(ident[:], 0.0).then_inc(sem("id0"), 1)
            nc.gpsimd.memset(ones[:], 1.0).then_inc(sem("id0"), 1)
            nc.gpsimd.iota(grid[:], [[1, GRID]], base=0, channel_multiplier=0,
                           allow_small_or_imprecise_dtypes=True).then_inc(sem("id0"), 1)
            pool.wait_ge(sem("id0"), 3)
            nc.gpsimd.affine_select(out=ident[:], in_=ident[:], compare_op=ALU.not_equal, fill=1.0, base=0,
                                    pattern=[[-1, P]], channel_multiplier=1).then_inc(sem("ident"), 1)
            nc.gpsimd.iota(key_col, [[0, 1]], base=P, channel_multiplier=1,
                           allow_small_or_imprecise_dtypes=True).then_inc(sem("key_col"), 1)
            pool.wait_ge(sem("key_col"), 1)
            pool.wait_ge(sem("ident"), 1)
            pool.wait_ge(sem("split0"), 1)
            for t in range(T):
                ins = nc.gpsimd.tensor_scalar(key_diag[:, t, :], ident[:], key_col, float(2 ** t), ALU.mult, ALU.mult)
            ins.then_inc(sem("key_diag"), 1)
            with pool.Fori(0, T // 2) as b:
                for u in range(2):
                    pool.wait_ge(sem("v"), b * 2 + u + 1)
                    pool.dma_start(table[bass.ds((b * 2 + u) * P, P), :], vring[:, u, :]
                                   ).then_inc(sem(f"v_stored{u}"), 16)
            pool.wait_ge(sem("agg0"), T)
            nc.gpsimd.memset(tri, 0.0).then_inc(sem("tri0"), 1)
            pool.wait_ge(sem("tri0"), 1)
            pool.dma_start(table[N:N + 1, :], tri[0:1, :]).then_inc(sem("zero_row"), 16)
            pool.dma_start(list_dram[0:N].rearrange("(p t) o -> p (t o)", p=P), tri[:, 0:T].bitcast(I32)
                           ).then_inc(sem("zero_row"), 16)
            pool.wait_ge(sem("zero_row"), 32)
            nc.gpsimd.affine_select(out=tri, in_=tri, compare_op=ALU.is_ge, fill=1.0, base=0,
                                    pattern=[[-1, P]], channel_multiplier=1).then_inc(sem("tri"), 1)
            nc.gpsimd.iota(ids, [[P, T]], base=0, channel_multiplier=1).then_inc(sem("ids"), 1)
            pool.wait_ge(sem("flag"), 1)
            nc.gpsimd.partition_all_reduce(tile_max[:, 0, :], seen, P, RMAX).then_inc(sem("tile_max"), 1)
            nc.gpsimd.partition_all_reduce(tile_max[:, 1, :], flag, P, RADD).then_inc(sem("tile_max"), 1)
            pool.wait_ge(sem("ids"), 1)
            pool.wait_ge(sem("pos"), 1)
            for i in range(T):
                pool.indirect_dma_start(list_dram, bass.IndirectOffsetOnAxis(pos[:, i:i + 1].bitcast(U32), 0),
                                        ids[:, i:i + 1], None).then_inc(sem("row_put"), 16)
            for u in range(2):
                pool.wait_ge(sem(f"v_stored{u}"), 16 * (T // 2))
            with pool.Fori(0, T) as i:
                turns = pool.value_load(control[0:1, 0, bass.ds(i, 1)], min_val=1, max_val=KEEP // GATHERS)
                before = pool.value_load(control[0:1, 1, bass.ds(i, 1)], min_val=0, max_val=T * KEEP // GATHERS)
                with pool.Fori(0, turns) as k:
                    turn = before + k
                    for half in range(2):
                        h = GATHERS // 2
                        pool.wait_ge(sem("used"), turn * GATHERS + half * h + h)
                        nc.gpsimd.tensor_copy(index_now[:, half * h:(half + 1) * h],
                                              index[:, bass.ds(i, 1), bass.ds(k * GATHERS + half * h, h)].rearrange(
                                                  "p o k -> p (o k)")).then_inc(sem("index_now"), 1)
                        wait_reg(pool, sem("index_now"), turn * 2 + half + 1)
                        for s in range(half * h, (half + 1) * h):
                            pool.indirect_dma_start(gathered[:, s, :], None, table,
                                                    bass.IndirectOffsetOnAxis(index_now[:, s:s + 1].bitcast(U32), 0)
                                                    ).then_inc(sem(f"gathered{s}"), 16)
            pool.wait_ge(sem("unit"), J)
            for j in range(J):
                for t in range(T):
                    pool.wait_ge(sem("pv1"), j * T + t + 1)
                    nc.gpsimd.tensor_scalar(work[:, t % 4, :], inv_bc[:, j * NB:(j + 1) * NB], neg_eps_inv[:, t:t + 1], 1.0,
                                            ALU.mult, ALU.add).then_inc(sem("den1"), 1)
            pool.wait_ge(sem("trange"), 1)
            nc.gpsimd.partition_all_reduce(trange[:, 4:8], trange[:, 0:4], P, RMAX).then_inc(sem("trange_all"), 1)

        @block.scalar
        def _(act):
            act_front(act, "0", ht0)
            act_features(act, "0", ring0, gs)
            act.sem_inc(sem("cast"), STAGES)
            with act.Fori(0, QB) as b:
                for q in range(QT):
                    act.wait_ge(sem(f"adj_in{q % STAGES}"), b * (16 * (QT // STAGES)) + 16 * (q // STAGES) + 16)
                    nc.scalar.activation(adj_u8[:, q * TQ:(q + 1) * TQ, bass.ds(b * NQ, NQ)], stage[:, q % STAGES],
                                         ACT.Copy, scale=ONE8).then_inc(sem("cast"), 1)
            act.sem_inc(sem("vt"), 2)
            with act.Fori(0, J // 2) as g2:
                for u in range(2):
                    act.wait_ge(sem("vt_ps"), g2 * 2 + u + 1)
                    nc.scalar.activation(blk(vt, g2 * 2 + u), ps[:, u, :], ACT.Copy).then_inc(sem("vt"), 1)

            act.wait_ge(sem("rows_in"), 16)
            act.wait_ge(sem("control"), 1)
            count = act.value_load(control[0:1, 2, T - 1:T], min_val=0, max_val=N)
            with act.If(count > 0):
                with act.Fori(0, count) as r:
                    n = act.value_load(rows_list[:, bass.ds(r, 1)], min_val=0, max_val=N - 1)
                    act.wait_ge(sem("mask"), r * 2 + 2)
                    nc.scalar.activation(column[:], adj_u8[:, :, bass.ds(n, 1)].rearrange("p t o -> p (t o)"),
                                         ACT.Copy, scale=1.0 / ONE8).then_inc(sem("column"), 1)

            act_front(act, "1", ht)
            act.sem_inc(sem("hp"), 2)
            with act.Fori(0, J // 2) as g2:
                for u in range(2):
                    act.wait_ge(sem("hp_ps"), g2 * 2 + u + 1)
                    nc.scalar.activation(hp[:, bass.ds(g2 * 8 + u * 4, 4), 0:F],
                                         ps[:, 2 + u].rearrange("p (k f) -> p k f", f=F), ACT.Copy
                                         ).then_inc(sem("hp"), 1)
            act.wait_ge(sem("sumsq"), 1)
            nc.scalar.activation(normp, normp, ACT.Sqrt).then_inc(sem("normp"), 1)
            act.sem_inc(sem("sumsq_bc"), 2)
            with act.Fori(0, J // 2) as g2:
                for u in range(2):
                    act.wait_ge(sem("sumsq_bc"), g2 * 2 + u + 1)
                    nc.scalar.activation(work[:, u, :], blk(ht, g2 * 2 + u), ACT.Square).then_inc(sem("sq"), 1)
                    act.wait_ge(sem("sumsq_bc"), g2 * 2 + u + 3)
                    nc.scalar.activation(blk(inv_bc, g2 * 2 + u), ps[:, u, :], ACT.Sqrt).then_inc(sem("norm_bc"), 1)
            nc.scalar.preload_act_table(ACT.Exp)
            act.wait_ge(sem("beta"), 1)
            with act.Fori(0, J) as j:
                with act.Fori(0, T // 4) as tt:
                    for u in range(4):
                        act.wait_ge(sem("cos1"), j * T + tt * 4 + u + 5)
                        nc.scalar.activation(work[:, u, :], work[:, u, :], ACT.Exp, bias=nbeta, scale=beta_col
                                             ).then_inc(sem("exp1"), 1)
            act_front(act, "2", ht)
            act.wait_ge(sem("deg1"), 1)
            nc.scalar.activation(degs, degs, ACT.Sqrt).then_inc(sem("deg_sqrt"), 1)
            nc.scalar.activation(degp, degp, ACT.Sqrt).then_inc(sem("deg_sqrt"), 1)
            act_features(act, "2", work, gs2)
            act_front(act, "3", ht)
            act.sem_inc(sem("cp"), 2)
            with act.Fori(0, T // 4) as g2:
                for u in range(2):
                    t0 = g2 * 4 + u * 2
                    act.wait_ge(sem("cp_ps"), g2 * 2 + u + 1)
                    src = ps[:, 2 + u, 0:2 * (F + 2)].rearrange("p (k f) -> p k f", f=F + 2)
                    dst = cp[:, bass.ds(t0, 2), :, 0:FH]
                    for k in range(2):
                        nc.scalar.activation(cp[:, bass.ds(t0 + k, 1), :, 0:FH].rearrange("p o h f -> p (o h) f"),
                                             src[:, k, 0:F].rearrange("p (h f) -> p h f", h=HEADS), ACT.Copy)
                    nc.scalar.activation(tneigh[:, bass.ds(t0, 2), :], src[:, :, F:F + 2], ACT.Copy
                                         ).then_inc(sem("cp"), 1)
            nc.scalar.preload_act_table(ACT.Exp)
            with act.Fori(0, J) as j:
                for h in range(HEADS):
                    act.wait_ge(sem("s_ps"), j * HEADS + h + 1)
                    if h == 0:
                        act.wait_ge(sem("x3b"), j + 1)
                    nc.scalar.activation(rows[:, 0, h, :], ps[:, 1 + h, :], ACT.Copy).then_inc(sem("s_row"), 1)
                for h in range(HEADS):
                    act.wait_ge(sem("zmax"), j * HEADS + h + 1)
                    nc.scalar.activation(rows[:, 1, h, :], rows[:, 2, h, :], ACT.Exp).then_inc(sem("ezmax"), 1)
                act.wait_ge(sem("m_row"), j + 1)
                with act.Fori(0, T // 2) as tt:
                    for u in range(2):
                        g = j * T + tt * 2 + u
                        act.wait_ge(sem("pv3"), g + 1)
                        for h in range(HEADS):
                            nc.scalar.activation(work[:, 2 * u + h, :], rows[:, 0, h, :], ACT.Exp,
                                                 bias=tile(tneigh, tt * 2 + u)[:, h:h + 1]).then_inc(sem("ez3"), 1)
                    for u in range(2):
                        for h in range(HEADS):
                            act.wait_ge(sem("score3"), j * (T * 2) + tt * 4 + u * 2 + h + 1)
                            nc.scalar.activation(work[:, 2 * u + h, :], work[:, 2 * u + h, :], ACT.Exp
                                                 ).then_inc(sem("exp3"), 1)

        @block.tensor
        def _(pe):
            pe.wait_ge(sem("ident"), 1)
            pe_front(pe, "0", ring0)
            pe.wait_ge(sem("w_in"), 16 * 6)
            pe_features(pe, "0", ht0, w0s[:])
            pe.wait_ge(sem("split0"), 1)
            for b in range(QB):
                pe.wait_ge(sem("cast"), b * QT + STAGES + QT)
                for u in range(2):
                    i = b * 2 + u
                    pe_aggregate(pe, i, u, "0", gs, 3 * F + 1, i + 1)
                    if i == 0:
                        pe.wait_ge(sem("key_diag"), 1)
                    for k in range(CHUNKS):
                        if i * CHUNKS + k >= 4:
                            pe.wait_ge(sem("ranked"), i * CHUNKS + k - 3)
                        for t in range(CHUNK):
                            tt = k * CHUNK + t
                            ins = nc.tensor.matmul(ps[:, 4 + k % 4, t * P:(t + 1) * P], adj8[:, tt, i * P:(i + 1) * P],
                                                   key_diag[:, tt, :], start=True, stop=True)
                        ins.then_inc(sem("key_ps"), 1)
            pe.wait_ge(sem("tri"), 1)
            pe.wait_ge(sem("flag"), 1)
            nc.tensor.matmul(ps[:, 2, 0:T], tri, flag, start=True, stop=True).then_inc(sem("rank"), 1)
            pe.wait_ge(sem("tp_in"), 16)
            pe.wait_ge(sem("agg0_used"), 2 + T)
            for g2 in range(J // 2):
                for u in range(2):
                    pe.wait_ge(sem("vt"), g2 * 2 + u + 1)
                    for k in range(4):
                        ins = nc.tensor.transpose(ps[:, u, k * P:(k + 1) * P], tile(tp, g2 * 8 + u * 4 + k), ident[:])
                    ins.then_inc(sem("vt_ps"), 1)
            pe.wait_ge(sem("vt"), 2 + J)
            pe.sem_inc(sem("mask"), 2)
            pe.wait_ge(sem("control"), 1)
            pe.wait_ge(sem("ranked"), CHUNKS * T)
            count = pe.value_load(control[0:1, 2, T - 1:T], min_val=0, max_val=N)
            with pe.If(count > 0):
                with pe.Fori(0, count) as r:
                    pe.wait_ge(sem("column"), r + 1)
                    for half in range(2):
                        pe.wait_ge(sem("mask_used"), r * 2 + half + 1)
                        for t in range(T // 2):
                            tt = half * (T // 2) + t
                            ins = nc.tensor.matmul(ps[:, 4 * half + t // 4, (t % 4) * P:(t % 4 + 1) * P],
                                                   column[:, tt:tt + 1].to_broadcast([P, P]), ident_bf[:],
                                                   start=True, stop=True)
                        ins.then_inc(sem("mask"), 1)
            pe.wait_ge(sem("pooled"), 1)
            for g2 in range(J // 2):
                for u in range(2):
                    pe.wait_ge(sem("x0"), g2 * 2 + u + 1)
                    for k in range(4):
                        ins = nc.tensor.transpose(ps[:, u, k * P:(k + 1) * P], blk(dt_, g2 * 8 + u * 4 + k, P), ident[:])
                    ins.then_inc(sem("pooled_ps"), 1)

            pe_front(pe, "1", work)
            pe.wait_ge(sem("ht1"), 2 + J)
            for g2 in range(J // 2):
                for u in range(2):
                    pe.wait_ge(sem("hp"), g2 * 2 + u + 1)
                    for k in range(4):
                        ins = nc.tensor.transpose(ps[:, 2 + u, k * F:(k + 1) * F], spread(ht, g2 * 8 + u * 4 + k), ident[:])
                    ins.then_inc(sem("hp_ps"), 1)
            with pe.Fori(0, J // 2) as g2:
                for u in range(2):
                    pe.wait_ge(sem("sq"), g2 * 2 + u + 1)
                    nc.tensor.matmul(ps[:, u, :], ones[:], work[:, u, :], start=True, stop=True
                                     ).then_inc(sem("sumsq_bc"), 1)
            pe.wait_ge(sem("unit"), J)
            pe.wait_ge(sem("hp"), 2 + J)
            pe.sem_inc(sem("pv1"), 4)

            def dots(j, t, u, g):
                pe.wait_ge(sem("cos1"), g + 1)
                nc.tensor.matmul(ps[:, u, :], spread(ht, t), blk(ht, j), start=True, stop=True).then_inc(sem("dot1"), 1)

            def weigh(t, u, g, first, last):
                pe.wait_ge(sem("prob1"), g + 1)
                for s in range(4):
                    ins = nc.tensor.matmul(ps[:, 4 + s, 0:F + 1], work[:, u, s * P:(s + 1) * P], tile(hp, t)[:, 0:F + 1],
                                           start=first, stop=last)
                ins.then_inc(sem("pv1"), 1)

            def block1(j, last_block):
                pe.wait_ge(sem("x1b"), j + 1)
                for t in range(T):
                    weigh(t, t % 4, j * T + t, t == 0, t == T - 1)
                    if t + 4 < T:
                        dots(j, t + 4, t % 4, j * T + t + 4)
                    elif not last_block:
                        dots(j + 1, t + 4 - T, t % 4, j * T + t + 4)

            for u in range(4):
                dots(0, u, u, u)
            with pe.Fori(0, J - 1) as j:
                block1(j, False)
            block1(J - 1, True)

            pe_front(pe, "2", work)
            pe_features(pe, "2", ht, w2s[:])
            pe.wait_ge(sem("split2"), 1)
            for b in range(T // 2):
                for u in range(2):
                    pe_aggregate(pe, b * 2 + u, u, "2", gs2, 3 * F, b * 2 + u + 1)

            pe_front(pe, "3", work)
            pe.wait_ge(sem("ht3"), 2 + J)
            pe.wait_ge(sem("att"), 1)
            for g2 in range(T // 4):
                for u in range(2):
                    pe.wait_ge(sem("cp"), g2 * 2 + u + 1)
                    for k in range(2):
                        ins = nc.tensor.matmul(ps[:, 2 + u, k * (F + 2):(k + 1) * (F + 2)],
                                               spread(ht, g2 * 4 + u * 2 + k), k3s[:], start=True, stop=True)
                    ins.then_inc(sem("cp_ps"), 1)
            pe.wait_ge(sem("cp"), 2 + T // 2)
            pe.wait_ge(sem("ind"), 1)
            for j in range(J):
                if j >= 2:
                    pe.wait_ge(sem("over_raw"), j - 1)
                for t in range(T):
                    ins = nc.tensor.matmul(ps[:, j % 2, :], ind[:, t, :], adj8[:, t, j * NB:(j + 1) * NB],
                                           start=(t == 0), stop=(t == T - 1))
                ins.then_inc(sem("cnt"), 1)
            pe.wait_ge(sem("over"), 1)
            pe.sem_inc(sem("pv3"), 2)
            with pe.Fori(0, J) as j:
                pe.wait_ge(sem("x3b"), j + 1)
                for h in range(HEADS):
                    nc.tensor.matmul(ps[:, 1 + h, :], s_w[h], blk(ht, j), start=True, stop=True).then_inc(sem("s_ps"), 1)
                pe.wait_ge(sem("over_j"), j + 1)
                for h in range(HEADS):
                    nc.tensor.matmul(ps[:, 3 * (1 - h), :], head_ones[:, h, :], over_j, start=True, stop=True
                                     ).then_inc(sem("steps"), 1)

                def weigh3(tt, first, last):
                    for u in range(2):
                        pe.wait_ge(sem("prob3"), j * (T * 2) + tt * 4 + u * 2 + 2)
                        for s in range(4):
                            for h in range(HEADS):
                                ins = nc.tensor.matmul(ps[:, 4 + s, h * (FH + 1):(h + 1) * (FH + 1)],
                                                       work[:, 2 * u + h, s * P:(s + 1) * P],
                                                       cp[:, bass.ds(tt * 2 + u, 1), h, :].rearrange("p o f -> p (o f)"),
                                                       start=(first and u == 0 and h == 0),
                                                       stop=(last and u == 1 and h == 1), skip_group_check=True)
                        ins.then_inc(sem("pv3"), 1)

                weigh3(0, True, False)
                with pe.Fori(1, T // 2 - 1) as tt:
                    weigh3(tt, False, False)
                weigh3(T // 2 - 1, False, True)

        @block.vector
        def _(dve):
            c = Tally(sem("dve_chain"))
            c.up(nc.vector.memset(zero_col, 0.0))
            dve.wait_ge(sem("ident"), 1)
            c.up(nc.vector.tensor_copy(ident_bf[:], ident[:]))
            dve.wait_ge(sem("x0_in"), 16)
            dve_front(dve, c, "0", x0, ring0)
            dve_features(dve, c, "0", ring0, gs, None)
            dve.wait_ge(sem("w_in"), 16 * 6)
            dve.sem_inc(sem("agg0_used"), 2)

            def activate0(b, stored):
                for u in range(2):
                    i = b * 2 + u
                    dve.wait_ge(sem("agg0"), i + 1)
                    if stored is not None:
                        dve.wait_ge(sem(f"v_stored{u}"), stored)
                    c.up(nc.vector.tensor_reduce(vring[:, u, :], ps[:, u, 0:3 * F].rearrange("p (s f) -> p f s", s=3),
                                                 AX_X, ALU.add))
                    nc.vector.tensor_copy(col(degs, i), ps[:, u, 3 * F:3 * F + 1]).then_inc(sem("agg0_used"), 1)
                    c.wait(dve)
                    c.up(nc.vector.tensor_tensor(vring[:, u, :], vring[:, u, :], b0s[:], ALU.add))
                    c.wait(dve)
                    nc.vector.tensor_scalar(vring[:, u, :], vring[:, u, :], 0.0, None, ALU.max).then_inc(sem("v"), 1)
                    for k in range(CHUNKS):
                        wait_reg(dve, sem("key_ps"), i * CHUNKS + k + 1)
                        nc.vector.max(slots[:, u, k * 8:(k + 1) * 8], ps[:, 4 + k % 4, :]).then_inc(sem("ranked"), 1)
                    wait_reg(dve, sem("ranked"), i * CHUNKS + CHUNKS)
                    for k in range(KEEP // 8):
                        c.up(nc.vector.max(best[:, k * 8:(k + 1) * 8], slots[:, u, :]))
                        if k < KEEP // 8 - 1:
                            wait_reg(dve, c.sem, c.n)
                            c.up(nc.vector.match_replace(slots[:, u, :], best[:, k * 8:(k + 1) * 8], slots[:, u, :], 0.0))
                            wait_reg(dve, c.sem, c.n)
                    c.wait(dve)
                    c.up(nc.vector.tensor_copy(tile(keys, i), best))

            activate0(0, None)
            with looped(dve, T // 2 - 1, (c, 2 * (2 + 2 * (KEEP // 8)))) as b:
                activate0(b + 1, b * 16 + 16)
            dve.wait_ge(sem("agg0_used"), 2 + T)
            c.up(nc.vector.tensor_scalar(none, degs, 0.0, F32_MIN, ALU.is_equal, ALU.mult))
            allk = keys.rearrange("p i k -> p (i k)")
            f0 = tmp[0].bitcast(F32)
            c.wait(dve)
            c.up(nc.vector.tensor_scalar(f0, allk, 0.0, None, ALU.is_gt))
            c.wait(dve)
            c.up(nc.vector.tensor_reduce(cnt, f0.rearrange("p (i k) -> p i k", k=KEEP), AX_X, ALU.add))
            c.wait(dve)
            c.up(nc.vector.tensor_tensor(flag, cnt, degs, ALU.is_lt))
            c.wait(dve)
            c.up(nc.vector.tensor_tensor(seen, cnt, flag, ALU.mult))
            c.wait(dve)
            nc.vector.tensor_tensor(seen, cnt, seen, ALU.subtract).then_inc(sem("flag"), 1)
            flat = index.rearrange("p i k -> p (i k)")
            c.up(nc.vector.tensor_scalar(flat, allk.bitcast(I32), 16, 7, ALU.logical_shift_right,
                                         ALU.logical_shift_right))
            c.up(nc.vector.tensor_scalar(tmp[0], allk.bitcast(I32), 16, P - 1, ALU.logical_shift_right, ALU.bitwise_and))
            c.wait(dve)
            c.up(nc.vector.tensor_scalar(tmp[0], tmp[0], float(T), -float(KEY0 // P), ALU.mult, ALU.add))
            c.wait(dve)
            c.up(nc.vector.tensor_tensor(flat, flat, tmp[0], ALU.add))
            c.wait(dve)
            c.up(nc.vector.tensor_scalar(tmp[1], flat, 0.0, float(N + KEY0 // P), ALU.is_lt, ALU.mult))
            c.wait(dve)
            nc.vector.tensor_tensor(flat, flat, tmp[1], ALU.add).then_inc(sem("index"), 1)
            dve.wait_ge(sem("tile_max"), 2)
            c.up(nc.vector.tensor_scalar(control[:, 0, :], tile_max[:, 0, :], float(GATHERS - 1), None, ALU.add))
            c.wait(dve)
            c.up(nc.vector.tensor_scalar(control[:, 0, :], control[:, 0, :], GATHERS.bit_length() - 1, None,
                                         ALU.logical_shift_right))
            c.wait(dve)
            c.up(nc.vector.tensor_scalar(control[:, 0, :], control[:, 0, :], 1.0, None, ALU.max))
            c.wait(dve)
            c.up(nc.vector.tensor_copy(scan[:, 0, 0, :], control[:, 0, :]))
            c.up(nc.vector.tensor_copy(scan[:, 0, 1, :], tile_max[:, 1, :]))
            a, step = 0, 1
            while step < T:
                c.wait(dve)
                c.up(nc.vector.tensor_copy(scan[:, 1 - a, :, 0:step], scan[:, a, :, 0:step]))
                c.up(nc.vector.tensor_tensor(scan[:, 1 - a, :, step:T], scan[:, a, :, step:T], scan[:, a, :, 0:T - step],
                                             ALU.add))
                a, step = 1 - a, 2 * step
            c.wait(dve)
            c.up(nc.vector.tensor_copy(control[:, 3, :], scan[:, a, 0, :]))
            c.up(nc.vector.tensor_tensor(control[:, 1, :], scan[:, a, 0, :], control[:, 0, :], ALU.subtract))
            c.wait(dve)
            nc.vector.tensor_copy(control[:, 2, :], scan[:, a, 1, :]).then_inc(sem("control"), 1)
            c.up(nc.vector.tensor_tensor(posf, scan[:, a, 1, :], tile_max[:, 1, :], ALU.subtract))
            dve.wait_ge(sem("rank"), 1)
            c.wait(dve)
            c.up(nc.vector.tensor_tensor(posf, posf, ps[:, 2, 0:T], ALU.add))
            dve.wait_ge(sem("ids"), 1)
            c.up(nc.vector.tensor_scalar(cnt, ids, float(N), None, ALU.add))
            c.wait(dve)
            c.up(nc.vector.tensor_tensor(posf, posf, cnt, ALU.subtract))
            c.wait(dve)
            c.up(nc.vector.tensor_tensor(posf, posf, flag, ALU.mult))
            c.wait(dve)
            nc.vector.tensor_tensor(pos, posf, cnt, ALU.add).then_inc(sem("pos"), 1)
            c.up(nc.vector.memset(pooled, 0.0))
            dve.wait_ge(sem("vt"), 2 + J)
            c.up(nc.vector.memset(dt_, 0.0))
            c.wait(dve)
            dve.sem_inc(sem("mask_used"), 2)
            dve.sem_inc(sem("used"), GATHERS)
            dve.wait_ge(sem("rows_in"), 16)
            dense = dve.value_load(control[0:1, 2, T - 1:T], min_val=0, max_val=N)
            every = dve.value_load(control[0:1, 3, T - 1:T], min_val=1, max_val=T * KEEP // GATHERS)

            def dense_row(r):
                n = dve.value_load(rows_list[:, bass.ds(r, 1)], min_val=0, max_val=N - 1)
                for half in range(2):
                    if half:
                        dve.wait_ge(sem("mask_used"), r * 2 + 3)
                    wait_reg(dve, sem("mask"), r * 2 + half + 3)
                    nc.vector.tensor_tensor_reduce(junk, vt[:, half * HB:(half + 1) * HB],
                                                   ps[:, 4 * half:4 * half + 4, :].rearrange("p b n -> p (b n)"), 1.0,
                                                   rowmax if half else 0.0, ALU.mult, ALU.max,
                                                   rowmax2 if half else rowmax).then_inc(sem("mask_used"), 1)
                dve.wait_ge(sem("mask_used"), r * 2 + 4)
                nc.vector.tensor_copy(col(dt_, n), rowmax2).then_inc(sem("row_max"), 1)

            with dve.Fori(0, T) as i:
                turns = dve.value_load(control[0:1, 0, bass.ds(i, 1)], min_val=1, max_val=KEEP // GATHERS)
                before = dve.value_load(control[0:1, 1, bass.ds(i, 1)], min_val=0, max_val=T * KEEP // GATHERS)
                with dve.Fori(0, turns) as k:
                    turn = before + k
                    for s in range(GATHERS):
                        dve.wait_ge(sem(f"gathered{s}"), turn * 16 + 16)
                        dve.wait_ge(sem("used"), turn * GATHERS + GATHERS + s)
                        nc.vector.tensor_tensor(tile(pooled, i), tile(pooled, i), gathered[:, s, :], ALU.max
                                                ).then_inc(sem("used"), 1)
                    with dve.If(turn < dense):
                        dense_row(turn)
            with dve.If(dense > every):
                with dve.Fori(every, dense) as r:
                    dense_row(r)
            nc.vector.memset(zero_col, 0.0).then_inc(sem("pooled"), 1)
            dve.wait_ge(sem("xr_in"), 16)
            dve.sem_inc(sem("x0"), 2)
            with dve.Fori(0, J // 2) as g2:
                for u in range(2):
                    dve.wait_ge(sem("pooled_ps"), g2 * 2 + u + 1)
                    four = pooled[:, bass.ds(g2 * 8 + u * 4, 4), :].rearrange("p k f -> p (k f)")
                    nc.vector.tensor_tensor(four, four, ps[:, u, :], ALU.max).then_inc(sem("x0"), 1)
                    dve.wait_ge(sem("x0"), g2 * 2 + u + 3)
                    for k in range(4):
                        i = g2 * 8 + u * 4 + k
                        ins = nc.vector.scalar_tensor_tensor(tile(xr, i), tile(pooled, i), col(none, i),
                                                             tile(xr, i), ALU.add, ALU.add)
                    ins.then_inc(sem("x0_sum"), 1)
            dve.wait_ge(sem("x0_sum"), J)

            dve_front(dve, c, "1", xr, work)
            dve.wait_ge(sem("hp"), 2 + J)
            c.up(nc.vector.memset(hp[:, :, F], 1.0))
            for t in range(T):
                c.wait(dve)
                c.up(nc.vector.tensor_tensor_reduce(work[:, 3, 0:F], hp[:, t, 0:F], hp[:, t, 0:F], 1.0, 0.0,
                                                    ALU.mult, ALU.add, normp[:, t:t + 1]))
            c.wait(dve)
            nc.vector.memset(zero_col, 0.0).then_inc(sem("sumsq"), 1)
            c.up(nc.vector.tensor_scalar(nbeta, beta_col, -1.0, None, ALU.mult))
            c.wait(dve)
            nc.vector.tensor_tensor(nbeta, nbeta, beta_col, ALU.min).then_inc(sem("beta"), 1)
            dve.wait_ge(sem("normp"), 1)
            c.up(nc.vector.tensor_scalar(normp, normp, TINY, None, ALU.max))
            c.wait(dve)
            c.up(nc.vector.reciprocal(normp, normp))
            c.wait(dve)
            c.up(nc.vector.tensor_scalar(neg_eps_inv, normp, -COS_EPS, None, ALU.mult))
            with looped(dve, J, (c, 2)) as j:
                dve.wait_ge(sem("norm_bc"), j + 1)
                r = blk(inv_bc, j)
                c.up(nc.vector.tensor_scalar(r, r, TINY, None, ALU.max))
                wait_reg(dve, c.sem, c.n)
                c.up(nc.vector.reciprocal(r, r))
                c.wait(dve)
                nc.vector.tensor_tensor(blk(ht, j), blk(ht, j), r, ALU.mult).then_inc(sem("unit"), 1)
            dve.sem_inc(sem("cos1"), 4)
            dve.sem_inc(sem("x1b"), 1)
            with looped(dve, J, (c, 1)) as j:
                with dve.Fori(0, T // 4) as tt:
                    def cosines(u):
                        g = j * T + tt * 4 + u
                        w = work[:, u, :]
                        dve.wait_ge(sem("den1"), g + 1)
                        dve.wait_ge(sem("dot1"), g + 1)
                        nc.vector.tensor_tensor(w, w, ps[:, u, :], ALU.mult).then_inc(sem("cos1"), 1)

                    def masked(u):
                        w = work[:, u, :]
                        dve.wait_ge(sem("exp1"), j * T + tt * 4 + u + 1)
                        nc.vector.tensor_tensor(w, w, adj_u8[:, bass.ds(tt * 4 + u, 1), bass.ds(j * NB, NB)].rearrange(
                            "p o n -> p (o n)"), ALU.mult).then_inc(sem("prob1"), 1)

                    cosines(0)
                    cosines(1)
                    masked(0)
                    cosines(2)
                    masked(1)
                    cosines(3)
                    masked(2)
                    masked(3)
                dve.wait_ge(sem("pv1"), j * T + T + 4)
                c.up(nc.vector.reciprocal(rinv, ps[:, 4:8, F]))
                c.wait(dve)
                for s in range(4):
                    ins = nc.vector.scalar_tensor_tensor(tile(xr, j * 4 + s), ps[:, 4 + s, 0:F], rinv[:, s:s + 1],
                                                         tile(xr, j * 4 + s), ALU.mult, ALU.add)
                ins.then_inc(sem("x1b"), 1)
            dve.wait_ge(sem("x1b"), 1 + J)

            dve.wait_ge(sem("deg_in"), 16)
            for d in (degs, degp):
                c.up(nc.vector.tensor_scalar(d, d, 1.0, 1e-12, ALU.add, ALU.max))
            c.wait(dve)
            nc.vector.memset(zero_col, 0.0).then_inc(sem("deg1"), 1)
            dve_front(dve, c, "2", xr, work)
            dve.wait_ge(sem("deg_sqrt"), 2)
            for d in (degs, degp):
                c.up(nc.vector.reciprocal(d, d))
            c.wait(dve)
            for t in range(T):
                d = spread(adj8[:, t, :], t)
                c.up(nc.vector.tensor_tensor(d, d, ident[:], ALU.add, saturate=False))
            dve_features(dve, c, "2", work, gs2, degp)
            dve.sem_inc(sem("agg2_used"), 2)
            with looped(dve, T // 2, (c, 4)) as b:
                for u in range(2):
                    i = b * 2 + u
                    a = work[:, u, 0:F]
                    dve.wait_ge(sem("agg2"), i + 1)
                    nc.vector.tensor_reduce(a, ps[:, u, 0:3 * F].rearrange("p (s f) -> p f s", s=3), AX_X, ALU.add
                                            ).then_inc(sem("agg2_used"), 1)
                    dve.wait_ge(sem("agg2_used"), i + 3)
                    c.up(nc.vector.scalar_tensor_tensor(a, a, col(degs, i), b2s[:], ALU.mult, ALU.add))
                    c.wait(dve)
                    c.up(nc.vector.scalar_tensor_tensor(tile(xr, i), a, 0.0, tile(xr, i), ALU.max, ALU.add))
            c.wait(dve)
            nc.vector.memset(zero_col, 0.0).then_inc(sem("x2"), 1)
            for t in range(T):
                d = spread(adj8[:, t, :], t)
                c.up(nc.vector.tensor_tensor(d, d, ident[:], ALU.subtract, saturate=False))

            dve.wait_ge(sem("att_in"), 16)
            for h in range(HEADS):
                for which, dst in ((0, s_col[:, h:h + 1]), (1, k3s[:, F + h:F + h + 1])):
                    c.wait(dve)
                    c.up(nc.vector.tensor_tensor_reduce(work[:, 1, 0:FH], k3s[:, h * FH:(h + 1) * FH],
                                                        work[:, 0, h * F + which * FH:h * F + (which + 1) * FH],
                                                        1.0, 0.0, ALU.mult, ALU.add, dst))
            c.wait(dve)
            for h in range(HEADS):
                c.up(nc.vector.tensor_scalar(s_w[h], ones[:], s_col[:, h:h + 1], None, ALU.mult))
            for h in range(HEADS):
                c.up(nc.vector.memset(head_ones[:, h, :], 0.0))
                c.wait(dve)
                c.up(nc.vector.memset(head_ones[h * GRID:(h + 1) * GRID, h, :], 1.0))
            c.wait(dve)
            nc.vector.memset(zero_col, 0.0).then_inc(sem("att"), 1)
            dve_front(dve, c, "3", xr, work)
            dve.wait_ge(sem("cp"), 2 + T // 2)
            c.up(nc.vector.memset(cp[:, :, :, FH], 1.0))
            tv = tneigh.rearrange("p t h -> p h t")
            c.up(nc.vector.tensor_reduce(trange[:, 0:2], tv, AX_X, ALU.max))
            c.up(nc.vector.tensor_reduce(trange[:, 2:4], tv, AX_X, ALU.min))
            c.wait(dve)
            nc.vector.tensor_scalar(trange[:, 2:4], trange[:, 2:4], -1.0, None, ALU.mult).then_inc(sem("trange"), 1)
            dve.wait_ge(sem("trange_all"), 1)
            c.up(nc.vector.tensor_tensor(tstep, trange[:, 4:6], trange[:, 6:8], ALU.add))
            c.up(nc.vector.tensor_scalar(tmin, trange[:, 6:8], -1.0, None, ALU.mult))
            c.wait(dve)
            c.up(nc.vector.tensor_scalar(tstep, tstep, 1.0 / GRID, None, ALU.mult))
            c.wait(dve)
            for h in range(HEADS):
                c.up(nc.vector.tensor_scalar(theta[:, h, :], grid[:], tstep[:, h:h + 1], tmin[:, h:h + 1],
                                             ALU.mult, ALU.add))
            c.wait(dve)
            for t in range(T):
                for h in range(HEADS):
                    c.up(nc.vector.tensor_scalar(ind[:, t, :][:, h * GRID:(h + 1) * GRID], theta[:, h, :],
                                                 tile(tneigh, t)[:, h:h + 1], None, ALU.is_le, saturate=False))
            c.wait(dve)
            nc.vector.memset(zero_col, 0.0).then_inc(sem("ind"), 1)
            for j in range(J):
                dve.wait_ge(sem("cnt"), j + 1)
                nc.vector.tensor_scalar(over_raw[:, j * NB:(j + 1) * NB], ps[:, j % 2, :], 0.5, None, ALU.is_gt).then_inc(sem("over_raw"), 1)
            dve.wait_ge(sem("over_raw"), J)
            nc.vector.tensor_copy(view(49408, 4096, F32), view(53504, 4096, F32)).then_inc(sem("over"), 1)
            dve.wait_ge(sem("over"), 1)
            dve.sem_inc(sem("x3b"), 1)
            with looped(dve, J, (c, 8 + 2 * T + 1)) as j:
                nc.vector.tensor_copy(over_j, blk(over, j)).then_inc(sem("over_j"), 1)
                for h in range(HEADS):
                    dve.wait_ge(sem("steps"), j * HEADS + h + 1)
                    c.up(nc.vector.tensor_scalar(rows[:, 2, h, :], ps[:, 3 * (1 - h), :], tstep[:, h:h + 1],
                                                 tmin[:, h:h + 1], ALU.mult, ALU.add))
                    c.wait(dve)
                    dve.wait_ge(sem("s_row"), j * HEADS + h + 1)
                    nc.vector.tensor_tensor(rows[:, 2, h, :], rows[:, 2, h, :], rows[:, 0, h, :], ALU.add
                                            ).then_inc(sem("zmax"), 1)
                for h in range(HEADS):
                    s, a, m = (rows[:, r, h, :] for r in range(3))
                    dve.wait_ge(sem("ezmax"), j * HEADS + h + 1)
                    c.up(nc.vector.tensor_scalar(a, a, 1.0, -1.0, ALU.min, ALU.add))
                    c.wait(dve)
                    c.up(nc.vector.tensor_tensor(m, m, a, ALU.max))
                    c.wait(dve)
                    c.up(nc.vector.tensor_tensor(a, s, m, ALU.subtract))
                for h in range(HEADS):
                    ins = nc.vector.tensor_scalar(rows[:, 2, h, :], rows[:, 2, h, :], 1.0, None, ALU.add)
                ins.then_inc(sem("m_row"), 1)
                wait_reg(dve, sem("m_row"), j + 1)
                with looped(dve, T // 2, (c, 4)) as tt:
                    for u in range(2):
                        for h in range(HEADS):
                            w = work[:, 2 * u + h, :]
                            dve.wait_ge(sem("ez3"), j * (T * 2) + tt * 4 + u * 2 + h + 1)
                            c.up(nc.vector.scalar_tensor_tensor(w, w, 1.0, rows[:, 2, h, :], ALU.min, ALU.subtract))
                            c.wait(dve)
                            nc.vector.scalar_tensor_tensor(w, rows[:, 1, h, :], tile(tneigh, tt * 2 + u)[:, h:h + 1], w,
                                                           ALU.add, ALU.max).then_inc(sem("score3"), 1)
                    for u in range(2):
                        for h in range(HEADS):
                            w = work[:, 2 * u + h, :]
                            dve.wait_ge(sem("exp3"), j * (T * 2) + tt * 4 + u * 2 + h + 1)
                            nc.vector.scalar_tensor_tensor(w, w, 2.0, adj_u8[:, bass.ds(tt * 2 + u, 1),
                                                           bass.ds(j * NB, NB)].rearrange("p o n -> p (o n)"),
                                                           ALU.min, ALU.mult).then_inc(sem("prob3"), 1)
                dve.wait_ge(sem("pv3"), j * T + T + 2)
                for h in range(HEADS):
                    o = h * (FH + 1)
                    ins = nc.vector.reciprocal(rinv[:, 0:4] if h == 0 else rinv2, ps[:, 4:8, o + FH])
                c.up(ins)
                c.wait(dve)
                for s in range(4):
                    for h in range(HEADS):
                        o = h * (FH + 1)
                        xt = tile(xr, j * 4 + s)[:, h * FH:(h + 1) * FH]
                        r = (rinv if h == 0 else rinv2)[:, s:s + 1]
                        ins = nc.vector.scalar_tensor_tensor(xt, ps[:, 4 + s, o:o + FH], r, xt, ALU.mult, ALU.add)
                ins.then_inc(sem("x3b"), 1)
            dve.wait_ge(sem("x3b"), 1 + J)
            nc.vector.memset(zero_col, 0.0).then_inc(sem("x3"), 1)


def kernel(**inputs):
    import numpy as _np
    import concourse.bacc as _bacc
    from concourse import mybir as _mybir
    from concourse.bass_utils import run_bass_kernel_spmd as _run

    nc = _bacc.Bacc("TRN2", target_bir_lowering=False, num_devices=1)
    arrays = {
        "x_in": inputs["x"],
        "adj_t": _np.asarray(inputs["adj"]).T,
        "w0": inputs["L0_gnn_weight"],
        "b0": inputs["L0_gnn_bias"],
        "beta": inputs["L1_gnn_beta"],
        "w2t": _np.asarray(inputs["L2_gnn_W"]).T,
        "b2": inputs["L2_gnn_b"],
        "k3": inputs["L3_gnn_kernels"],
        "att": inputs["L3_gnn_att_kernels"],
    }
    arrays = {n: _np.ascontiguousarray(a) for n, a in arrays.items()}
    args = [nc.dram_tensor(n, a.shape, _mybir.dt.from_np(a.dtype), kind="ExternalInput").ap()
            for n, a in arrays.items()]
    out = nc.dram_tensor("out_0", (4096, 128), _mybir.dt.float32, kind="ExternalOutput").ap()
    build(nc, *args, out)
    r = _run(nc, [arrays], core_ids=[0])
    return r.results[0]["out_0"]
```

```python
from contextlib import ExitStack

import concourse.bass as bass
from concourse import mybir

P = 128
F = 128
N = 4096
T = N // P
HEADS = 2
FH = F // HEADS
NB = 512
J = N // NB
GRID = P // HEADS
CHUNK = 4
CHUNKS = T // CHUNK
KEEP = 32
KEY0 = 134 * P
GATHERS = 4
SAFE = 80.0
LN_EPS = 1e-5
COS_EPS = 1e-7
TINY = 1e-18
F32_MIN = -3.4028234663852886e38

ALU = mybir.AluOpType
ACT = mybir.ActivationFunctionType
F32 = mybir.dt.float32
BF16 = mybir.dt.bfloat16
FP8 = mybir.dt.float8e4
I32 = mybir.dt.int32
U32 = mybir.dt.uint32
U8 = mybir.dt.uint8
AX_X = mybir.AxisListType.X
RMAX = bass.bass_isa.ReduceOp.max
RADD = bass.bass_isa.ReduceOp.add



class Tally:

    def __init__(self, sem):
        self.sem, self.n = sem, 0

    def up(self, ins):
        ins.then_inc(self.sem, 1)
        self.n = self.n + 1
        return ins

    def wait(self, eng):
        eng.wait_ge(self.sem, self.n)


class looped:

    def __init__(self, eng, count, *tallies):
        self.eng, self.count, self.tallies = eng, count, tallies

    def __enter__(self):
        self.cm = self.eng.Fori(0, self.count)
        i = self.cm.__enter__()
        self.base = [t.n for t, _ in self.tallies]
        for (t, per), b in zip(self.tallies, self.base):
            t.n = i * per + b
        return i

    def __exit__(self, *exc):
        r = self.cm.__exit__(*exc)
        for (t, per), b in zip(self.tallies, self.base):
            t.n = b + self.count * per
        return r


def build(nc, x, adj_t, w0, b0, beta, w2t, b2, k3, att, out):
    with ExitStack() as ctx:
        def sb(name, shape, dt):
            return ctx.enter_context(nc.sbuf_tensor(name, shape, dt))

        sems = {}

        def sem(name):
            if name not in sems:
                sems[name] = ctx.enter_context(nc.semaphore(name))
            return sems[name]

        rows_dram = nc.dram_tensor("score_rows", (3, HEADS, N), F32).ap()
        list_dram = nc.dram_tensor("dense_rows", (2 * N, 1), I32).ap()
        table = nc.dram_tensor("v_table", (N + 1, F), F32).ap()
        deg_dram = nc.dram_tensor("deg_rows", (N,), F32).ap()

        adj8 = sb("adj8", [P, T, N], FP8)
        ONE8 = 56.0
        adj_u8 = adj8[:].bitcast(U8)
        arena = sb("arena", [P, 73984 // 4], F32)

        def view(at, nbytes, dt):
            v = arena[:, at // 4:(at + nbytes) // 4]
            return v if dt == F32 else v.bitcast(dt)

        SPLIT_W = 3 * F + 2
        CP_W = HEADS * (FH + 1)
        x0 = view(0, 16384, F32).rearrange("p (i f) -> p i f", f=F)
        ht0 = view(24704, 16384, F32)
        gs = view(0, 24704, BF16).rearrange("p (t c) -> p t c", c=SPLIT_W)
        ring0 = view(41088, 8192, F32).rearrange("p (b c) -> p b c", c=NB)
        STAGES, TQ, NQ = 4, 4, 256
        stage = view(49408, 16384, F32).rearrange("p (s t n) -> p s t n", s=STAGES, n=NQ)
        key_diag = view(41088, 8192, BF16).rearrange("p (t k) -> p t k", k=P)
        slots = view(65792, 512, F32).rearrange("p (b k) -> p b k", b=2)
        keys = view(25728, 4096, F32).rearrange("p (i k) -> p i k", k=KEEP)
        tmp = [view(b, 4096, I32) for b in (0, 4096)]
        tri = view(8192, 512, F32)
        flag = view(8704, 128, F32)
        cnt = view(8832, 128, F32)
        seen = view(8960, 128, F32)
        pos = view(9088, 128, I32)
        posf = view(9216, 128, F32)
        ids = view(9344, 128, I32)
        scan = view(9472, 512, F32).rearrange("p (b w i) -> p b w i", b=2, w=2)
        tile_max = view(9984, 256, F32).rearrange("p (w i) -> p w i", w=2)
        LIST_END = 16
        rows_list = view(0, 16384, I32)[0:1, :]
        pooled = view(16384, 16384, F32).rearrange("p (i f) -> p i f", f=F)
        index = view(65792, 4096, I32).rearrange("p (i k) -> p i k", k=KEEP)
        gathered = view(69888, 2048, F32).rearrange("p (s f) -> p s f", f=F)
        vring = view(24704, 1024, F32).rearrange("p (b f) -> p b f", b=2)
        xr = view(0, 16384, F32).rearrange("p (i f) -> p i f", f=F)
        ht = view(16384, 16384, F32)
        tp = view(32768, 16384, F32).rearrange("p (t f) -> p t f", f=F)
        dt_ = view(32768, 16384, F32)
        hp = view(32768, 16640, F32).rearrange("p (t c) -> p t c", c=130)
        gs2 = view(32768, 24704, BF16).rearrange("p (t c) -> p t c", c=SPLIT_W)
        vt = view(49408, 16384, F32)
        inv_bc = view(49408, 16384, F32)
        work = view(65792, 8192, F32).rearrange("p (b c) -> p b c", c=NB)
        junk = view(71936, 2048, U8)
        ind = view(49408, 4096, FP8).rearrange("p (t k) -> p t k", k=P)
        reach = view(53504, 2048, F32)
        rows = view(49408, 24576, F32).rearrange("p (b r h n) -> p b r h n", b=2, r=3, h=HEADS)
        work3 = view(16384, 16384, F32).rearrange("p (b h n) -> p b h n", h=HEADS, n=NB)

        ident = sb("ident", [P, P], F32)
        ident_bf = sb("ident_bf", [P, P], BF16)
        w0s = sb("w0s", [P, F], F32)
        w2s = sb("w2s", [P, F], F32)
        b0s = sb("b0s", [P, F], F32)
        b2s = sb("b2s", [P, F], F32)
        k3s = sb("k3s", [P, F + 2], F32)
        small = sb("small", [P, 512], F32)
        stats = small[:, 0:192].rearrange("p (i c) -> p i c", c=6)
        mv = small[:, 192:256].rearrange("p (i c) -> p i c", c=2)
        rstd = small[:, 256:288]
        degs = small[:, 288:320]
        degp = small[:, 320:352]
        none = small[:, 352:384]
        normp = small[:, 384:416]
        neg_eps_inv = rstd
        misc = small[:, 416:512]
        eps_col = misc[:, 0:1]
        beta_col = misc[:, 1:2]
        nbeta = misc[:, 2:3]
        rowmax = misc[:, 3:4]
        rinv = misc[:, 4:8]
        zero_col = misc[:, 8:9]
        rowmax2 = misc[:, 27:28]
        trange = misc[:, 9:17]
        tstep = misc[:, 17:19]
        tmin = misc[:, 19:21]
        rinv2 = misc[:, 21:25]
        s_col = misc[:, 25:27]
        tneigh = sb("tneigh", [P, T * HEADS], F32)[:].rearrange("p (t h) -> p t h", h=HEADS)
        control = sb("control", [P, 4, T], I32)
        index_now = sb("index_now", [P, GATHERS], I32)[:]
        best = view(66304, 128, F32)
        key_col = misc[:, 28:29]
        wide = misc[:, 29:30].bitcast(I32)
        range_max = misc[:, 30:31]
        column = view(49152, 64, BF16)
        grid = sb("grid", [P, GRID], F32)
        cols = small[:, 0:192].rearrange("p (r h i) -> p r h i", r=3, h=HEADS)
        steps = small[:, 192:256].rearrange("p (i h) -> p i h", h=HEADS)
        rowt = view(57344, 1024, F32).rearrange("p (r q) -> p r q", r=2)
        theta = b2s[:].rearrange("p (h k) -> p h k", h=HEADS)
        cp = view(32768, 16640, F32).rearrange("p (t h c) -> p t h c", h=HEADS, c=FH + 1)

        ps = ctx.enter_context(nc.psum_tensor("ps", [P, 8, NB], F32))

        x_rows = x.rearrange("(i q) f -> q i f", q=P)
        out_rows = out.rearrange("(i q) f -> q i f", q=P)
        adj_spread = adj_t.rearrange("(p t) n -> p t n", p=P)

        def spread(a, t, k=1):
            v = a.rearrange("f (p t) -> f t p", t=T)
            if isinstance(t, int) and k == 1:
                return v[:, t, :]
            return v[:, bass.ds(t, k), :].rearrange("f o p -> f (o p)")

        def spread4(a, g):
            return a.rearrange("f (p t) -> f t p", t=T)[:, bass.ds(g * 4, 4), :]

        def sums1(b, s):
            return ps[:, 4 + 2 * b + s // 2, s % 2 * (NB // 2):(s % 2 + 1) * (NB // 2)]

        QB = N // NQ
        QT = T // TQ
        HB = 4 * NB

        block = ctx.enter_context(nc.Block())

        def wait_reg(eng, s, value):
            eng.wait_ge(s, value)
            eng.sem_inc(sem("waits_passed"), 1)

        def tile(a, i):
            return a[:, bass.ds(i, 1), :].rearrange("p o f -> p (o f)")

        def col(a, i):
            return a[:, bass.ds(i, 1)]

        def blk(a, j, w=NB):
            return a[:, bass.ds(j * w, w)]

        @block.sync
        def _(sp):
            sp.dma_start(x0, x_rows).then_inc(sem("x0_in"), 16)
            for dst, src in ((w0s[:], w0), (w2s[:], w2t),
                             (k3s[:, 0:F].rearrange("p (h f) -> p h f", h=HEADS), k3.rearrange("h d f -> d h f")),
                             (b0s[:], b0.partition_broadcast(P)), (b2s[:], b2.partition_broadcast(P)),
                             (beta_col, beta.partition_broadcast(P))):
                sp.dma_start(dst, src).then_inc(sem("w_in"), 16)
            with sp.Fori(0, QB) as b:
                for q in range(QT):
                    sp.wait_ge(sem("cast"), b * QT + q + 1)
                    sp.dma_start(stage[:, q % STAGES], adj_spread[:, q * TQ:(q + 1) * TQ, bass.ds(b * NQ, NQ)]
                                 ).then_inc(sem(f"adj_in{q % STAGES}"), 16)
            sp.wait_ge(sem("agg0_used"), 2 + T)
            with nc.allow_non_contiguous_dma(reason="one word per node, once"):
                sp.dma_start(deg_dram.rearrange("(i q) -> q i", q=P), degs).then_inc(sem("deg_out"), 16)
            sp.wait_ge(sem("deg_out"), 16)
            sp.dma_start(degp, deg_dram.rearrange("(p t) -> p t", p=P)).then_inc(sem("deg_in"), 16)
            for u in range(2):
                sp.wait_ge(sem(f"v_stored{u}"), 16 * (T // 2))
            sp.wait_ge(sem("key_ps"), CHUNKS * T)
            sp.dma_start(tp, table[0:N].rearrange("(p t) f -> p t f", p=P)).then_inc(sem("tp_in"), 16)
            sp.wait_ge(sem("row_put"), 16 * T)
            sp.dma_start(rows_list, list_dram[0:N].rearrange("n o -> o n")).then_inc(sem("rows_in"), 16)
            sp.dma_start(xr[LIST_END:P], x_rows[LIST_END:P]).then_inc(sem("xr_in"), 16)
            sp.wait_ge(sem("pooled"), 1)
            sp.dma_start(xr[0:LIST_END], x_rows[0:LIST_END]).then_inc(sem("xr_in"), 16)
            sp.wait_ge(sem("x1b"), 2 + J)
            sp.dma_start(work[:, 2, 0:HEADS * F], att.rearrange("h f -> (h f)").partition_broadcast(P)
                         ).then_inc(sem("att_in"), 16)
            sp.wait_ge(sem("rowt"), 1)
            sp.dma_start(rows_dram[0:2].rearrange("r h (i q) -> (r h i) q", q=P), rowt[:, 0, :]
                         ).then_inc(sem("rows_out"), 16)
            sp.dma_start(rows_dram[2].rearrange("h (i q) -> (h i) q", q=P), rowt[2 * T:P, 1, :]
                         ).then_inc(sem("rows_out"), 16)
            sp.wait_ge(sem("rows_out"), 32)
            with sp.Fori(0, J // 2) as j2:
                for u in range(2):
                    sp.wait_ge(sem("x3b"), j2 * 2 + u + 1)
                    sp.dma_start(rows[:, u].rearrange("p r h n -> p (r h) n"),
                                 rows_dram.rearrange("r h n -> (r h) n")[:, bass.ds((j2 * 2 + u) * NB, NB)]
                                 .partition_broadcast(P)).then_inc(sem(f"rows_in{u}"), 16)
            sp.wait_ge(sem("x3"), 1)
            sp.dma_start(out_rows, xr).then_inc(sem("out_stored"), 16)
            sp.wait_ge(sem("out_stored"), 16)

        def moments(dve, c, src, tiles):
            c.wait(dve)
            for i in tiles:
                c.up(nc.vector.bn_stats(tile(stats, i), tile(src, i)))

        def dve_front(dve, c, tag, src, ring):
            c.wait(dve)
            for i in range(T):
                c.up(nc.vector.bn_aggr(mv[:, i, :], stats[:, i, :]))
            c.wait(dve)
            nc.vector.memset(eps_col, LN_EPS).then_inc(sem("var" + tag), 1)
            dve.wait_ge(sem("std" + tag), 1)
            c.up(nc.vector.reciprocal(rstd, rstd))
            c.wait(dve)
            with dve.Fori(0, J // 2) as g2:
                for u in range(2):
                    dve.wait_ge(sem("yt" + tag), g2 * 2 + u + 1)
                    for k in range(4):
                        i = g2 * 8 + u * 4 + k
                        ins = nc.vector.tensor_scalar(ring[:, u, k * F:(k + 1) * F], tile(src, i),
                                                      tile(mv, i)[:, 0:1], col(rstd, i), ALU.subtract, ALU.mult)
                    ins.then_inc(sem("y" + tag), 1)

        def pe_front(pe, tag, ring):
            pe.sem_inc(sem("yt" + tag), 2)
            with pe.Fori(0, J // 2) as g2:
                for u in range(2):
                    pe.wait_ge(sem("y" + tag), g2 * 2 + u + 1)
                    pe.wait_ge(sem("ht" + tag), g2 * 2 + u + 1)
                    for k in range(4):
                        ins = nc.tensor.transpose(ps[:, u, k * F:(k + 1) * F], ring[:, u, k * F:(k + 1) * F], ident[:])
                    ins.then_inc(sem("yt" + tag), 1)

        def act_front(act, tag, dst):
            act.sem_inc(sem("ht" + tag), 2)
            act.wait_ge(sem("var" + tag), 1)
            nc.scalar.activation(rstd, mv[:, :, 1], ACT.Sqrt, bias=eps_col).then_inc(sem("std" + tag), 1)
            with act.Fori(0, J // 2) as g2:
                for u in range(2):
                    act.wait_ge(sem("yt" + tag), g2 * 2 + u + 3)
                    nc.scalar.activation(blk(dst, g2 * 2 + u), ps[:, u, :], ACT.Relu).then_inc(sem("ht" + tag), 1)

        def pe_features(pe, tag, h, w):
            pe.wait_ge(sem("ht" + tag), 2 + J)
            for g2 in range(J // 2):
                for u in range(2):
                    pe.wait_ge(sem("g_read" + tag), g2 * 2 + u + 1)
                    for k in range(4):
                        ins = nc.tensor.matmul(ps[:, 2 + u, k * F:(k + 1) * F], spread(h, g2 * 8 + u * 4 + k), w,
                                               start=True, stop=True)
                    ins.then_inc(sem("g" + tag), 1)

        def act_features(act, tag, ring, dst, scale):
            act.wait_ge(sem("y" + tag), J)
            act.sem_inc(sem("g_read" + tag), 2)
            with act.Fori(0, J // 2) as g2:
                for u in range(2):
                    act.wait_ge(sem("g" + tag), g2 * 2 + u + 1)
                    act.wait_ge(sem("part3" + tag), g2 * 2 + u + 1)
                    if scale is None:
                        ins = nc.scalar.activation(ring[:, u], ps[:, 2 + u, :], ACT.Copy)
                    else:
                        for k in range(4):
                            ins = nc.scalar.activation(ring[:, u, k * F:(k + 1) * F], ps[:, 2 + u, k * F:(k + 1) * F],
                                                       ACT.Copy, scale=col(scale, g2 * 8 + u * 4 + k))
                    ins.then_inc(sem("g_read" + tag), 1)
                    act.wait_ge(sem("g_read" + tag), g2 * 2 + u + 3)
                    nc.scalar.activation(dst[:, bass.ds(g2 * 8 + u * 4, 4), 0:F],
                                         ring[:, u].rearrange("p (k f) -> p k f", f=F), ACT.Copy
                                         ).then_inc(sem("part1" + tag), 1)

        def dve_features(dve, c, tag, ring, dst):
            dve.sem_inc(sem("part3" + tag), 2)
            dve.wait_ge(sem("y" + tag), J)
            c.up(nc.vector.memset(dst[:, :, 3 * F], 1.0))
            with looped(dve, J // 2, (c, 4)) as g2:
                for u in range(2):
                    r = ring[:, u].rearrange("p (k f) -> p k f", f=F)
                    d = [dst[:, bass.ds(g2 * 8 + u * 4, 4), s * F:(s + 1) * F] for s in range(3)]
                    dve.wait_ge(sem("part1" + tag), g2 * 2 + u + 1)
                    c.up(nc.vector.tensor_tensor(r, r, d[0], ALU.subtract))
                    c.wait(dve)
                    c.up(nc.vector.tensor_copy(d[1], r))
                    c.wait(dve)
                    nc.vector.tensor_tensor(d[2], r, d[1], ALU.subtract).then_inc(sem("part3" + tag), 1)
            c.wait(dve)
            dve.wait_ge(sem("part3" + tag), 2 + J)
            nc.vector.memset(zero_col, 0.0).then_inc(sem("split" + tag), 1)

        def pe_aggregate(pe, i, u, tag, src, width, credit_wait):
            pe.wait_ge(sem("agg" + tag + "_used"), credit_wait)
            for t in range(T):
                ins = nc.tensor.matmul(ps[:, u, 0:width], adj8[:, t, i * P:(i + 1) * P], src[:, t, 0:width],
                                       start=(t == 0), stop=(t == T - 1))
            ins.then_inc(sem("agg" + tag), 1)

        @block.gpsimd
        def _(pool):
            nc.gpsimd.memset(ident[:], 0.0).then_inc(sem("id0"), 1)
            nc.gpsimd.iota(grid[:], [[1, GRID]], base=0, channel_multiplier=0,
                           allow_small_or_imprecise_dtypes=True).then_inc(sem("id0"), 1)
            pool.wait_ge(sem("id0"), 2)
            nc.gpsimd.affine_select(out=ident[:], in_=ident[:], compare_op=ALU.not_equal, fill=1.0, base=0,
                                    pattern=[[-1, P]], channel_multiplier=1).then_inc(sem("ident"), 1)
            nc.gpsimd.iota(key_col, [[0, 1]], base=P, channel_multiplier=1,
                           allow_small_or_imprecise_dtypes=True).then_inc(sem("key_col"), 1)
            with pool.Fori(0, T // 2) as b:
                for u in range(2):
                    pool.wait_ge(sem("v"), b * 2 + u + 1)
                    pool.dma_start(table[bass.ds((b * 2 + u) * P, P), :], vring[:, u, :]
                                   ).then_inc(sem(f"v_stored{u}"), 16)
            pool.wait_ge(sem("agg0"), T)
            nc.gpsimd.memset(tri, 0.0).then_inc(sem("tri0"), 1)
            pool.wait_ge(sem("tri0"), 1)
            pool.dma_start(table[N:N + 1, :], tri[0:1, :]).then_inc(sem("zero_row"), 16)
            pool.dma_start(list_dram[0:N].rearrange("(p t) o -> p (t o)", p=P), tri[:, 0:T].bitcast(I32)
                           ).then_inc(sem("zero_row"), 16)
            pool.wait_ge(sem("zero_row"), 32)
            nc.gpsimd.affine_select(out=tri, in_=tri, compare_op=ALU.is_ge, fill=1.0, base=0,
                                    pattern=[[-1, P]], channel_multiplier=1).then_inc(sem("tri"), 1)
            nc.gpsimd.iota(ids, [[P, T]], base=0, channel_multiplier=1).then_inc(sem("ids"), 1)
            pool.wait_ge(sem("flag"), 1)
            nc.gpsimd.partition_all_reduce(tile_max[:, 0, :], seen, P, RMAX).then_inc(sem("tile_max"), 1)
            nc.gpsimd.partition_all_reduce(tile_max[:, 1, :], flag, P, RADD).then_inc(sem("tile_max"), 1)
            pool.wait_ge(sem("ids"), 1)
            pool.wait_ge(sem("pos"), 1)
            for i in range(T):
                pool.indirect_dma_start(list_dram, bass.IndirectOffsetOnAxis(pos[:, i:i + 1].bitcast(U32), 0),
                                        ids[:, i:i + 1], None).then_inc(sem("row_put"), 16)
            for u in range(2):
                pool.wait_ge(sem(f"v_stored{u}"), 16 * (T // 2))
            pool.wait_ge(sem("index"), 1)
            pool.wait_ge(sem("control"), 1)
            with pool.Fori(0, T) as i:
                turns = pool.value_load(control[0:1, 0, bass.ds(i, 1)], min_val=1, max_val=KEEP // GATHERS)
                before = pool.value_load(control[0:1, 1, bass.ds(i, 1)], min_val=0, max_val=T * KEEP // GATHERS)
                with pool.Fori(0, turns) as k:
                    turn = before + k
                    for half in range(2):
                        h = GATHERS // 2
                        pool.wait_ge(sem("used"), turn * GATHERS + half * h + h)
                        nc.gpsimd.tensor_copy(index_now[:, half * h:(half + 1) * h],
                                              index[:, bass.ds(i, 1), bass.ds(k * GATHERS + half * h, h)].rearrange(
                                                  "p o k -> p (o k)")).then_inc(sem("index_now"), 1)
                        wait_reg(pool, sem("index_now"), turn * 2 + half + 1)
                        for s in range(half * h, (half + 1) * h):
                            pool.indirect_dma_start(gathered[:, s, :], None, table,
                                                    bass.IndirectOffsetOnAxis(index_now[:, s:s + 1].bitcast(U32), 0)
                                                    ).then_inc(sem(f"gathered{s}"), 16)
            pool.wait_ge(sem("inv_bc"), 2 + J)
            pool.wait_ge(sem("neg_eps_inv"), 1)
            for j in range(J):
                for t in range(T):
                    pool.wait_ge(sem("pv1"), j * T + t + 1)
                    nc.gpsimd.tensor_scalar(work[:, t % 4, :], inv_bc[:, j * NB:(j + 1) * NB], neg_eps_inv[:, t:t + 1], 1.0,
                                            ALU.mult, ALU.add).then_inc(sem("den1"), 1)
            pool.wait_ge(sem("trange"), 1)
            nc.gpsimd.partition_all_reduce(trange[:, 4:8], trange[:, 0:4], P, RMAX).then_inc(sem("trange_all"), 1)
            def masks(bounded):
                for g in range(J * T):
                    for h in range(HEADS):
                        w = work3[:, g % 4, h, :]
                        pool.wait_ge(sem(f"exp3_{h}"), g + 1)
                        if bounded:
                            nc.gpsimd.tensor_scalar(w, w, 2.0, 0.0, ALU.min, ALU.max).then_inc(sem("bound3"), 1)
                            pool.wait_ge(sem("bound3"), g * HEADS + h + 1)
                        nc.gpsimd.tensor_tensor(w, w, adj8[:, g % T, g // T * NB:(g // T + 1) * NB], ALU.mult
                                                ).then_inc(sem(f"prob3_{h}"), 1)

            pool.wait_ge(sem("wide"), 1)
            is_wide = pool.value_load(wide[0:1, :], min_val=0, max_val=1)
            with pool.If(is_wide > 0):
                masks(True)
            with pool.If(is_wide < 1):
                masks(False)

        @block.scalar
        def _(act):
            act.sem_inc(sem("cast"), STAGES)
            def casts0(q0, q1):
                for q in range(q0, q1):
                    act.wait_ge(sem(f"adj_in{q % STAGES}"), 16 * (q // STAGES) + 16)
                    nc.scalar.activation(adj_u8[:, q * TQ:(q + 1) * TQ, 0:NQ], stage[:, q % STAGES],
                                         ACT.Copy, scale=ONE8).then_inc(sem("cast"), 1)

            casts0(0, QT // 2)
            act_front(act, "0", ht0)
            act_features(act, "0", ring0, gs, None)
            casts0(QT // 2, QT)
            with act.Fori(1, QB) as b:
                for q in range(QT):
                    act.wait_ge(sem(f"adj_in{q % STAGES}"), b * (16 * (QT // STAGES)) + 16 * (q // STAGES) + 16)
                    nc.scalar.activation(adj_u8[:, q * TQ:(q + 1) * TQ, bass.ds(b * NQ, NQ)], stage[:, q % STAGES],
                                         ACT.Copy, scale=ONE8).then_inc(sem("cast"), 1)
            act.sem_inc(sem("vt"), 2)
            with act.Fori(0, J // 2) as g2:
                for u in range(2):
                    act.wait_ge(sem("vt_ps"), g2 * 2 + u + 1)
                    nc.scalar.activation(blk(vt, g2 * 2 + u), ps[:, u, :], ACT.Copy).then_inc(sem("vt"), 1)

            act.wait_ge(sem("rows_in"), 16)
            act.wait_ge(sem("control"), 1)
            count = act.value_load(control[0:1, 2, T - 1:T], min_val=0, max_val=N)
            with act.If(count > 0):
                with act.Fori(0, count) as r:
                    n = act.value_load(rows_list[:, bass.ds(r, 1)], min_val=0, max_val=N - 1)
                    act.wait_ge(sem("mask"), r * 2 + 2)
                    nc.scalar.activation(column[:], adj_u8[:, :, bass.ds(n, 1)].rearrange("p t o -> p (t o)"),
                                         ACT.Copy, scale=1.0 / ONE8).then_inc(sem("column"), 1)

            act_front(act, "1", ht)
            act.sem_inc(sem("hp"), 2)
            with act.Fori(0, J // 2) as g2:
                for u in range(2):
                    act.wait_ge(sem("hp_ps"), g2 * 2 + u + 1)
                    nc.scalar.activation(hp[:, bass.ds(g2 * 8 + u * 4, 4), 0:F],
                                         ps[:, 2 + u].rearrange("p (k f) -> p k f", f=F), ACT.Copy
                                         ).then_inc(sem("hp"), 1)
            act.wait_ge(sem("sumsq"), 1)
            nc.scalar.activation(normp, normp, ACT.Sqrt).then_inc(sem("normp"), 1)
            act.sem_inc(sem("inv_bc"), 2)
            with act.Fori(0, J // 2) as g2:
                for u in range(2):
                    act.wait_ge(sem("inv_ps"), g2 * 2 + u + 1)
                    nc.scalar.activation(spread4(inv_bc, g2 * 2 + u), ps[:, u, :].rearrange("p (k q) -> p k q", k=4),
                                         ACT.Copy).then_inc(sem("inv_bc"), 1)
            nc.scalar.preload_act_table(ACT.Exp)
            act.wait_ge(sem("beta"), 1)
            with act.Fori(0, J) as j:
                with act.Fori(0, T // 4) as tt:
                    for u in range(4):
                        act.wait_ge(sem("cos1"), j * T + tt * 4 + u + 5)
                        nc.scalar.activation(work[:, u, :], work[:, u, :], ACT.Exp, bias=nbeta, scale=beta_col
                                             ).then_inc(sem("exp1"), 1)
            act_front(act, "2", ht)
            act.wait_ge(sem("deg1"), 1)
            nc.scalar.activation(degs, degs, ACT.Sqrt).then_inc(sem("deg_sqrt"), 1)
            nc.scalar.activation(degp, degp, ACT.Sqrt).then_inc(sem("deg_sqrt"), 1)
            act.wait_ge(sem("deg_inv"), 1)
            act_features(act, "2", work, gs2, degp)
            act_front(act, "3", ht)
            act.sem_inc(sem("cp"), 2)
            with act.Fori(0, T // 4) as g2:
                for u in range(2):
                    t0 = g2 * 4 + u * 2
                    act.wait_ge(sem("cp_ps"), g2 * 2 + u + 1)
                    src = ps[:, 2 + u, 0:2 * (F + 2)].rearrange("p (k f) -> p k f", f=F + 2)
                    for k in range(2):
                        nc.scalar.activation(cp[:, bass.ds(t0 + k, 1), :, 0:FH].rearrange("p o h f -> p (o h) f"),
                                             src[:, k, 0:F].rearrange("p (h f) -> p h f", h=HEADS), ACT.Copy)
                    nc.scalar.activation(tneigh[:, bass.ds(t0, 2), :], src[:, :, F:F + 2], ACT.Copy
                                         ).then_inc(sem("cp"), 1)
            nc.scalar.preload_act_table(ACT.Exp)
            act.wait_ge(sem("zmax"), 1)
            nc.scalar.activation(cols[:, 1], cols[:, 2], ACT.Exp).then_inc(sem("ezmax"), 1)
            act.wait_ge(sem("cols_ps"), 1)
            nc.scalar.activation(rowt, ps[:, 5, 0:2 * P].rearrange("p (r q) -> p r q", r=2), ACT.Copy
                                 ).then_inc(sem("rowt"), 1)

            def ez(j, b, t, u):
                for h in range(HEADS):
                    act.wait_ge(sem(f"pv3_{h}"), j * T + t + 1)
                    ins = nc.scalar.activation(work3[:, u, h, :], rows[:, b, 0, h, :], ACT.Exp,
                                               bias=tile(tneigh, t)[:, h:h + 1])
                ins.then_inc(sem("ez3"), 1)

            def weights(j, t, u):
                for h in range(HEADS):
                    act.wait_ge(sem(f"score3_{h}"), j * T + t + 1)
                    nc.scalar.activation(work3[:, u, h, :], work3[:, u, h, :], ACT.Exp
                                         ).then_inc(sem(f"exp3_{h}"), 1)

            def rows_ready(j, b):
                act.wait_ge(sem(f"rows_in{b}"), (j - b) * 8 + 16)

            def block3(j, b, last):
                with act.Fori(0, T // 4 - 1) as tt:
                    for u in range(4):
                        ez(j, b, tt * 4 + u + 2, (u + 2) % 4)
                        weights(j, tt * 4 + u, u)
                for u in range(4):
                    if u < 2:
                        ez(j, b, T - 2 + u, u + 2)
                    elif not last:
                        if u == 2:
                            rows_ready(j + 1, 1 - b)
                        ez(j + 1, 1 - b, u - 2, u - 2)
                    weights(j, T - 4 + u, u)

            rows_ready(0, 0)
            ez(0, 0, 0, 0)
            ez(0, 0, 1, 1)
            with act.Fori(0, J // 2 - 1) as j2:
                for b in range(2):
                    block3(j2 * 2 + b, b, False)
            block3(J - 2, 0, False)
            block3(J - 1, 1, True)

        @block.tensor
        def _(pe):
            pe.wait_ge(sem("ident"), 1)
            pe_front(pe, "0", ring0)
            pe.wait_ge(sem("w_in"), 16 * 6)
            pe_features(pe, "0", ht0, w0s[:])
            pe.wait_ge(sem("split0"), 1)
            def aggregate0(i, t0, t1):
                if t0 == 0:
                    if i % (NQ // P) == 0:
                        pe.wait_ge(sem("cast"), i // (NQ // P) * QT + STAGES + QT)
                    pe.wait_ge(sem("agg0_used"), i + 1)
                for t in range(t0, t1):
                    ins = nc.tensor.matmul(ps[:, i % 2, 0:3 * F + 1], adj8[:, t, i * P:(i + 1) * P], gs[:, t, 0:3 * F + 1],
                                           start=(t == 0), stop=(t == T - 1))
                if t1 == T:
                    ins.then_inc(sem("agg0"), 1)

            aggregate0(0, 0, T)
            pe.wait_ge(sem("key_diag"), 1)
            for i in range(T):
                for k in range(CHUNKS):
                    if i * CHUNKS + k >= 4:
                        pe.wait_ge(sem("ranked"), i * CHUNKS + k - 3)
                    for t in range(CHUNK):
                        tt = k * CHUNK + t
                        ins = nc.tensor.matmul(ps[:, 4 + k % 4, t * P:(t + 1) * P], adj8[:, tt, i * P:(i + 1) * P],
                                               key_diag[:, tt, :], start=True, stop=True)
                    ins.then_inc(sem("key_ps"), 1)
                    if i + 1 < T:
                        aggregate0(i + 1, k * CHUNK, (k + 1) * CHUNK)
            pe.wait_ge(sem("tri"), 1)
            pe.wait_ge(sem("flag"), 1)
            nc.tensor.matmul(ps[:, 2, 0:T], tri, flag, start=True, stop=True).then_inc(sem("rank"), 1)
            pe.wait_ge(sem("tp_in"), 16)
            pe.wait_ge(sem("agg0_used"), 2 + T)
            for g2 in range(J // 2):
                for u in range(2):
                    pe.wait_ge(sem("vt"), g2 * 2 + u + 1)
                    for k in range(4):
                        ins = nc.tensor.transpose(ps[:, u, k * P:(k + 1) * P], tile(tp, g2 * 8 + u * 4 + k), ident[:])
                    ins.then_inc(sem("vt_ps"), 1)
            pe.wait_ge(sem("vt"), 2 + J)
            pe.sem_inc(sem("mask"), 2)
            pe.wait_ge(sem("control"), 1)
            pe.wait_ge(sem("ranked"), CHUNKS * T)
            count = pe.value_load(control[0:1, 2, T - 1:T], min_val=0, max_val=N)
            with pe.If(count > 0):
                with pe.Fori(0, count) as r:
                    pe.wait_ge(sem("column"), r + 1)
                    for half in range(2):
                        pe.wait_ge(sem("mask_used"), r * 2 + half + 1)
                        for t in range(T // 2):
                            tt = half * (T // 2) + t
                            ins = nc.tensor.matmul(ps[:, 4 * half + t // 4, (t % 4) * P:(t % 4 + 1) * P],
                                                   column[:, tt:tt + 1].to_broadcast([P, P]), ident_bf[:],
                                                   start=True, stop=True)
                        ins.then_inc(sem("mask"), 1)
            pe.wait_ge(sem("pooled"), 1)
            for g2 in range(J // 2):
                for u in range(2):
                    pe.wait_ge(sem("x0"), g2 * 2 + u + 1)
                    for k in range(4):
                        ins = nc.tensor.transpose(ps[:, u, k * P:(k + 1) * P], blk(dt_, g2 * 8 + u * 4 + k, P), ident[:])
                    ins.then_inc(sem("pooled_ps"), 1)

            pe_front(pe, "1", work)
            pe.wait_ge(sem("ht1"), 2 + J)
            for g2 in range(J // 2):
                for u in range(2):
                    pe.wait_ge(sem("hp"), g2 * 2 + u + 1)
                    for k in range(4):
                        ins = nc.tensor.transpose(ps[:, 2 + u, k * F:(k + 1) * F], spread(ht, g2 * 8 + u * 4 + k), ident[:])
                    ins.then_inc(sem("hp_ps"), 1)
            pe.wait_ge(sem("inv"), 1)
            for g in range(J):
                pe.wait_ge(sem("inv_bc"), g + 1)
                for k in range(4):
                    ins = nc.tensor.matmul(ps[:, g % 2, k * P:(k + 1) * P],
                                           normp[:, g * 4 + k:g * 4 + k + 1].to_broadcast([P, P]), ident[:],
                                           start=True, stop=True)
                ins.then_inc(sem("inv_ps"), 1)
            pe.wait_ge(sem("unit"), J)
            pe.wait_ge(sem("hp"), 2 + J)
            pe.sem_inc(sem("pv1"), 4)

            def dots(j, t, u, g):
                pe.wait_ge(sem("cos1"), g + 1)
                nc.tensor.matmul(ps[:, u, :], spread(ht, t), blk(ht, j), start=True, stop=True).then_inc(sem("dot1"), 1)

            def weigh(b, t, u, g, first, last):
                pe.wait_ge(sem("prob1"), g + 1)
                for s in range(4):
                    ins = nc.tensor.matmul(sums1(b, s)[:, 0:F + 1], work[:, u, s * P:(s + 1) * P], tile(hp, t)[:, 0:F + 1],
                                           start=(first and s % 2 == 0), stop=(last and s % 2 == 1),
                                           skip_group_check=True)
                ins.then_inc(sem("pv1"), 1)

            def block1(j, b, last_block=False):
                pe.wait_ge(sem("x1b"), j + 1)
                for t in range(T):
                    weigh(b, t, t % 4, j * T + t, t == 0, t == T - 1)
                    if t + 4 < T:
                        dots(j, t + 4, t % 4, j * T + t + 4)
                    elif not last_block:
                        dots(j + 1, t + 4 - T, t % 4, j * T + t + 4)

            for u in range(4):
                dots(0, u, u, u)
            with pe.Fori(0, J // 2 - 1) as j2:
                for b in range(2):
                    block1(j2 * 2 + b, b)
            block1(J - 2, 0)
            block1(J - 1, 1, last_block=True)

            pe_front(pe, "2", work)
            pe_features(pe, "2", ht, w2s[:])
            pe.wait_ge(sem("split2"), 1)
            for b in range(T // 2):
                for u in range(2):
                    pe_aggregate(pe, b * 2 + u, u, "2", gs2, 3 * F, b * 2 + u + 1)

            pe_front(pe, "3", work)
            pe.wait_ge(sem("ht3"), 2 + J)
            pe.wait_ge(sem("att"), 1)
            for g2 in range(T // 4):
                for u in range(2):
                    pe.wait_ge(sem("cp"), g2 * 2 + u + 1)
                    for k in range(2):
                        ins = nc.tensor.matmul(ps[:, 2 + u, k * (F + 2):(k + 1) * (F + 2)],
                                               spread(ht, g2 * 4 + u * 2 + k), k3s[:], start=True, stop=True)
                    ins.then_inc(sem("cp_ps"), 1)
            for i in range(T):
                ins = nc.tensor.matmul(ps[:, 4, 2 * i:2 * i + 2], ht[:, i * P:(i + 1) * P], s_col, start=True, stop=True)
            ins.then_inc(sem("s_ps"), 1)
            pe.wait_ge(sem("cp"), 2 + T // 2)
            pe.wait_ge(sem("ind"), 1)
            for g in range(J):
                if g >= 2:
                    pe.wait_ge(sem("reach"), g - 1)
                for k in range(4):
                    i = g * 4 + k
                    for t in range(T):
                        ins = nc.tensor.matmul(ps[:, g % 2, k * P:(k + 1) * P], adj8[:, t, i * P:(i + 1) * P], ind[:, t, :],
                                               start=(t == 0), stop=(t == T - 1))
                ins.then_inc(sem("cnt"), 1)
            pe.wait_ge(sem("cols"), 1)
            for r in range(2):
                ins = nc.tensor.transpose(ps[:, 5, r * P:(r + 1) * P],
                                          cols[:, r:r + 2].rearrange("p r h i -> p (r h i)"), ident[:])
            ins.then_inc(sem("cols_ps"), 1)
            pe.wait_ge(sem("rowt"), 1)
            for h in range(HEADS):
                pe.sem_inc(sem(f"pv3_{h}"), 4)

            def weigh3(j, b, t, u, first, last):
                for h in range(HEADS):
                    pe.wait_ge(sem(f"prob3_{h}"), j * T + t + 1)
                    for s in range(4):
                        ins = nc.tensor.matmul(ps[:, 4 * b + s, h * CP_W:(h + 1) * CP_W],
                                               work3[:, u, h, s * P:(s + 1) * P],
                                               cp[:, bass.ds(t, 1), :, :].rearrange("p o h f -> p (o h f)"),
                                               start=(first and h == 0), stop=(last and h == 1), skip_group_check=True)
                    ins.then_inc(sem(f"pv3_{h}"), 1)

            with pe.Fori(0, J // 2) as j2:
                for b in range(2):
                    j = j2 * 2 + b
                    pe.wait_ge(sem("x3b"), j + 1)
                    for u in range(4):
                        weigh3(j, b, u, u, u == 0, False)
                    with pe.Fori(1, T // 4 - 1) as tt:
                        for u in range(4):
                            weigh3(j, b, tt * 4 + u, u, False, False)
                    for u in range(4):
                        weigh3(j, b, T - 4 + u, u, False, u == 3)

        @block.vector
        def _(dve):
            c = Tally(sem("dve_chain"))
            c.up(nc.vector.memset(zero_col, 0.0))
            dve.wait_ge(sem("ident"), 1)
            c.up(nc.vector.tensor_copy(ident_bf[:], ident[:]))
            dve.wait_ge(sem("x0_in"), 16)
            moments(dve, c, x0, range(T))
            dve_front(dve, c, "0", x0, ring0)
            dve_features(dve, c, "0", ring0, gs)
            dve.wait_ge(sem("key_col"), 1)
            dve.wait_ge(sem("split0"), 1)
            for t in range(T):
                ins = nc.vector.tensor_scalar(key_diag[:, t, :], ident[:], key_col, float(2 ** t), ALU.mult, ALU.mult)
            ins.then_inc(sem("key_diag"), 1)
            dve.wait_ge(sem("w_in"), 16 * 6)
            dve.sem_inc(sem("agg0_used"), 2)

            m = Tally(sem("match_chain"))

            def add0(i, u, stored, step):
                v = vring[:, u, :]
                if step == 0:
                    dve.wait_ge(sem("agg0"), i + 1)
                    if stored is not None:
                        dve.wait_ge(sem(f"v_stored{u}"), stored)
                    c.up(nc.vector.tensor_reduce(v, ps[:, u, 0:3 * F].rearrange("p (s f) -> p f s", s=3), AX_X, ALU.add))
                    nc.vector.tensor_copy(col(degs, i), ps[:, u, 3 * F:3 * F + 1]).then_inc(sem("agg0_used"), 1)
                elif step == 1:
                    c.wait(dve)
                    c.up(nc.vector.tensor_tensor(v, v, b0s[:], ALU.add))
                else:
                    c.wait(dve)
                    nc.vector.tensor_scalar(v, v, 0.0, None, ALU.max).then_inc(sem("v"), 1)

            def keep(i, u, k):
                if k == 0:
                    wait_reg(dve, sem("ranked"), i * CHUNKS + CHUNKS)
                if k == 2 * (KEEP // 8) - 1:
                    m.wait(dve)
                    m.up(nc.vector.tensor_copy(tile(keys, i), best))
                    return
                if k or not isinstance(i, int) or i:
                    wait_reg(dve, m.sem, m.n)
                eight = best[:, k // 2 * 8:(k // 2 + 1) * 8]
                if k % 2 == 0:
                    m.up(nc.vector.max(eight, slots[:, u, :]))
                else:
                    m.up(nc.vector.match_replace(slots[:, u, :], eight, slots[:, u, :], 0.0))

            def rank0(i, u, stored, first=False):
                for k in range(CHUNKS):
                    wait_reg(dve, sem("key_ps"), i * CHUNKS + k + 1)
                    nc.vector.max(slots[:, u, k * 8:(k + 1) * 8], ps[:, 4 + k % 4, :]).then_inc(sem("ranked"), 1)
                    if not first:
                        keep(i - 1, 1 - u, k)
                    if 2 <= k < 5:
                        add0(i, u, stored, k - 2)

            rank0(0, 0, None, True)
            rank0(1, 1, None)
            with looped(dve, T // 2 - 1, (c, 4), (m, 4 * (KEEP // 8))) as b:
                rank0(b * 2 + 2, 0, b * 16 + 16)
                rank0(b * 2 + 3, 1, b * 16 + 16)
            for k in range(2 * (KEEP // 8)):
                keep(T - 1, 1, k)
            m.wait(dve)
            dve.wait_ge(sem("agg0_used"), 2 + T)
            c.up(nc.vector.tensor_scalar(none, degs, 0.0, F32_MIN, ALU.is_equal, ALU.mult))
            allk = keys.rearrange("p i k -> p (i k)")
            f0 = tmp[0].bitcast(F32)
            c.wait(dve)
            c.up(nc.vector.tensor_scalar(f0, allk, 0.0, None, ALU.is_gt))
            c.wait(dve)
            c.up(nc.vector.tensor_reduce(cnt, f0.rearrange("p (i k) -> p i k", k=KEEP), AX_X, ALU.add))
            c.wait(dve)
            c.up(nc.vector.tensor_tensor(flag, cnt, degs, ALU.is_lt))
            c.wait(dve)
            c.up(nc.vector.tensor_tensor(seen, cnt, flag, ALU.mult))
            c.wait(dve)
            nc.vector.tensor_tensor(seen, cnt, seen, ALU.subtract).then_inc(sem("flag"), 1)
            flat = index.rearrange("p i k -> p (i k)")
            c.up(nc.vector.tensor_scalar(flat, allk.bitcast(I32), 16, 7, ALU.logical_shift_right,
                                         ALU.logical_shift_right))
            c.up(nc.vector.tensor_scalar(tmp[0], allk.bitcast(I32), 16, P - 1, ALU.logical_shift_right, ALU.bitwise_and))
            c.wait(dve)
            c.up(nc.vector.tensor_scalar(tmp[0], tmp[0], float(T), -float(KEY0 // P), ALU.mult, ALU.add))
            c.wait(dve)
            c.up(nc.vector.tensor_tensor(flat, flat, tmp[0], ALU.add))
            c.wait(dve)
            c.up(nc.vector.tensor_scalar(tmp[1], flat, 0.0, float(N + KEY0 // P), ALU.is_lt, ALU.mult))
            c.wait(dve)
            nc.vector.tensor_tensor(flat, flat, tmp[1], ALU.add).then_inc(sem("index"), 1)
            dve.wait_ge(sem("tile_max"), 2)
            c.up(nc.vector.tensor_scalar(control[:, 0, :], tile_max[:, 0, :], float(GATHERS - 1), None, ALU.add))
            c.wait(dve)
            c.up(nc.vector.tensor_scalar(control[:, 0, :], control[:, 0, :], GATHERS.bit_length() - 1, None,
                                         ALU.logical_shift_right))
            c.wait(dve)
            c.up(nc.vector.tensor_scalar(control[:, 0, :], control[:, 0, :], 1.0, None, ALU.max))
            c.wait(dve)
            c.up(nc.vector.tensor_copy(scan[:, 0, 0, :], control[:, 0, :]))
            c.up(nc.vector.tensor_copy(scan[:, 0, 1, :], tile_max[:, 1, :]))
            a, step = 0, 1
            while step < T:
                c.wait(dve)
                c.up(nc.vector.tensor_copy(scan[:, 1 - a, :, 0:step], scan[:, a, :, 0:step]))
                c.up(nc.vector.tensor_tensor(scan[:, 1 - a, :, step:T], scan[:, a, :, step:T], scan[:, a, :, 0:T - step],
                                             ALU.add))
                a, step = 1 - a, 2 * step
            c.wait(dve)
            c.up(nc.vector.tensor_copy(control[:, 3, :], scan[:, a, 0, :]))
            c.up(nc.vector.tensor_tensor(control[:, 1, :], scan[:, a, 0, :], control[:, 0, :], ALU.subtract))
            c.wait(dve)
            nc.vector.tensor_copy(control[:, 2, :], scan[:, a, 1, :]).then_inc(sem("control"), 1)
            c.up(nc.vector.tensor_tensor(posf, scan[:, a, 1, :], tile_max[:, 1, :], ALU.subtract))
            dve.wait_ge(sem("rank"), 1)
            c.wait(dve)
            c.up(nc.vector.tensor_tensor(posf, posf, ps[:, 2, 0:T], ALU.add))
            dve.wait_ge(sem("ids"), 1)
            c.up(nc.vector.tensor_scalar(cnt, ids, float(N), None, ALU.add))
            c.wait(dve)
            c.up(nc.vector.tensor_tensor(posf, posf, cnt, ALU.subtract))
            c.wait(dve)
            c.up(nc.vector.tensor_tensor(posf, posf, flag, ALU.mult))
            c.wait(dve)
            nc.vector.tensor_tensor(pos, posf, cnt, ALU.add).then_inc(sem("pos"), 1)
            c.up(nc.vector.memset(pooled, 0.0))
            dve.wait_ge(sem("vt"), 2 + J)
            c.up(nc.vector.memset(dt_, 0.0))
            c.wait(dve)
            dve.sem_inc(sem("mask_used"), 2)
            dve.sem_inc(sem("used"), GATHERS)
            dve.wait_ge(sem("rows_in"), 16)
            dense = dve.value_load(control[0:1, 2, T - 1:T], min_val=0, max_val=N)
            every = dve.value_load(control[0:1, 3, T - 1:T], min_val=1, max_val=T * KEEP // GATHERS)

            def dense_half(r, half):
                if half:
                    dve.wait_ge(sem("mask_used"), r * 2 + 3)
                wait_reg(dve, sem("mask"), r * 2 + half + 3)
                nc.vector.tensor_tensor_reduce(junk, vt[:, half * HB:(half + 1) * HB],
                                               ps[:, 4 * half:4 * half + 4, :].rearrange("p b n -> p (b n)"), 1.0,
                                               rowmax if half else 0.0, ALU.mult, ALU.max,
                                               rowmax2 if half else rowmax).then_inc(sem("mask_used"), 1)
                if half:
                    n = dve.value_load(rows_list[:, bass.ds(r, 1)], min_val=0, max_val=N - 1)
                    dve.wait_ge(sem("mask_used"), r * 2 + 4)
                    nc.vector.tensor_copy(col(dt_, n), rowmax2).then_inc(sem("row_max"), 1)

            with dve.Fori(0, T) as i:
                turns = dve.value_load(control[0:1, 0, bass.ds(i, 1)], min_val=1, max_val=KEEP // GATHERS)
                before = dve.value_load(control[0:1, 1, bass.ds(i, 1)], min_val=0, max_val=T * KEEP // GATHERS)
                with dve.Fori(0, turns) as k:
                    turn = before + k
                    r = turn >> 1
                    for s in range(GATHERS):
                        dve.wait_ge(sem(f"gathered{s}"), turn * 16 + 16)
                        dve.wait_ge(sem("used"), turn * GATHERS + GATHERS + s)
                        nc.vector.tensor_tensor(tile(pooled, i), tile(pooled, i), gathered[:, s, :], ALU.max
                                                ).then_inc(sem("used"), 1)
                        if s == GATHERS // 2 - 1:
                            with dve.If(turn < dense * 2):
                                with dve.If((turn & 1) < 1):
                                    dense_half(r, 0)
                                with dve.If((turn & 1) > 0):
                                    dense_half(r, 1)
            with dve.If(dense * 2 > every):
                with dve.If((every & 1) > 0):
                    dense_half(every >> 1, 1)
                with dve.Fori((every + 1) >> 1, dense) as r:
                    dense_half(r, 0)
                    dense_half(r, 1)
            nc.vector.memset(zero_col, 0.0).then_inc(sem("pooled"), 1)
            dve.wait_ge(sem("xr_in"), 32)
            dve.sem_inc(sem("x0"), 2)
            with dve.Fori(0, J // 2) as g2:
                for u in range(2):
                    dve.wait_ge(sem("pooled_ps"), g2 * 2 + u + 1)
                    four = pooled[:, bass.ds(g2 * 8 + u * 4, 4), :].rearrange("p k f -> p (k f)")
                    nc.vector.tensor_tensor(four, four, ps[:, u, :], ALU.max).then_inc(sem("x0"), 1)
                    dve.wait_ge(sem("x0"), g2 * 2 + u + 3)
                    for k in range(4):
                        i = g2 * 8 + u * 4 + k
                        ins = nc.vector.scalar_tensor_tensor(tile(xr, i), tile(pooled, i), col(none, i),
                                                             tile(xr, i), ALU.add, ALU.add)
                    ins.then_inc(sem("x0_sum"), 1)
            dve.wait_ge(sem("x0_sum"), J)

            moments(dve, c, xr, range(T))
            dve_front(dve, c, "1", xr, work)
            dve.wait_ge(sem("hp"), 2 + J)
            c.up(nc.vector.memset(hp[:, :, F], 1.0))
            for t in range(T):
                c.wait(dve)
                c.up(nc.vector.tensor_tensor_reduce(work[:, 3, 0:F], hp[:, t, 0:F], hp[:, t, 0:F], 1.0, 0.0,
                                                    ALU.mult, ALU.add, normp[:, t:t + 1]))
            c.wait(dve)
            nc.vector.memset(zero_col, 0.0).then_inc(sem("sumsq"), 1)
            c.up(nc.vector.tensor_scalar(nbeta, beta_col, -1.0, None, ALU.mult))
            c.wait(dve)
            nc.vector.tensor_tensor(nbeta, nbeta, beta_col, ALU.min).then_inc(sem("beta"), 1)
            dve.wait_ge(sem("normp"), 1)
            c.up(nc.vector.tensor_scalar(normp, normp, TINY, None, ALU.max))
            c.wait(dve)
            c.up(nc.vector.reciprocal(normp, normp))
            c.wait(dve)
            nc.vector.tensor_scalar(neg_eps_inv, normp, -COS_EPS, None, ALU.mult).then_inc(sem("neg_eps_inv"), 1)
            nc.vector.memset(zero_col, 0.0).then_inc(sem("inv"), 1)
            with dve.Fori(0, J // 2) as g2:
                for u in range(2):
                    dve.wait_ge(sem("inv_bc"), g2 * 2 + u + 3)
                    four = spread4(ht, g2 * 2 + u)
                    nc.vector.tensor_tensor(four, four, spread4(inv_bc, g2 * 2 + u), ALU.mult).then_inc(sem("unit"), 1)
            dve.sem_inc(sem("cos1"), 4)
            dve.sem_inc(sem("x1b"), 2)

            def four_tiles(j, tt):
                def cosines(u):
                    g = j * T + tt * 4 + u
                    w = work[:, u, :]
                    dve.wait_ge(sem("den1"), g + 1)
                    dve.wait_ge(sem("dot1"), g + 1)
                    nc.vector.tensor_tensor(w, w, ps[:, u, :], ALU.mult).then_inc(sem("cos1"), 1)

                def masked(u):
                    w = work[:, u, :]
                    dve.wait_ge(sem("exp1"), j * T + tt * 4 + u + 1)
                    nc.vector.tensor_tensor(w, w, adj_u8[:, bass.ds(tt * 4 + u, 1), bass.ds(j * NB, NB)].rearrange(
                        "p o n -> p (o n)"), ALU.mult).then_inc(sem("prob1"), 1)

                cosines(0)
                cosines(1)
                masked(0)
                cosines(2)
                masked(1)
                cosines(3)
                masked(2)
                masked(3)

            def finish1(j, b):
                dve.wait_ge(sem("pv1"), j * T + T + 4)
                for s in range(4):
                    ins = nc.vector.reciprocal(rinv[:, s:s + 1], sums1(b, s)[:, F:F + 1])
                c.up(ins)
                c.wait(dve)
                for s in range(4):
                    ins = nc.vector.scalar_tensor_tensor(tile(xr, j * 4 + s), sums1(b, s)[:, 0:F], rinv[:, s:s + 1],
                                                         tile(xr, j * 4 + s), ALU.mult, ALU.add)
                ins.then_inc(sem("x1b"), 1)
                dve.wait_ge(sem("x1b"), j + 3)
                moments(dve, c, xr, [j * 4 + s for s in range(4)])

            def rest1(j):
                with dve.Fori(1, T // 4) as tt:
                    four_tiles(j, tt)

            four_tiles(0, 0)
            rest1(0)
            with looped(dve, J // 2 - 1, (c, 10)) as j2:
                for b in (1, 0):
                    j = j2 * 2 + 2 - b
                    four_tiles(j, 0)
                    finish1(j - 1, 1 - b)
                    rest1(j)
            four_tiles(J - 1, 0)
            finish1(J - 2, 0)
            rest1(J - 1)
            finish1(J - 1, 1)

            dve.wait_ge(sem("deg_in"), 16)
            for d in (degs, degp):
                c.up(nc.vector.tensor_scalar(d, d, 1.0, 1e-12, ALU.add, ALU.max))
            c.wait(dve)
            nc.vector.memset(zero_col, 0.0).then_inc(sem("deg1"), 1)
            dve_front(dve, c, "2", xr, work)
            dve.wait_ge(sem("deg_sqrt"), 2)
            for d in (degs, degp):
                c.up(nc.vector.reciprocal(d, d))
            c.wait(dve)
            nc.vector.memset(zero_col, 0.0).then_inc(sem("deg_inv"), 1)
            for t in range(T):
                d = spread(adj8[:, t, :], t)
                c.up(nc.vector.tensor_tensor(d, d, ident[:], ALU.add, saturate=False))
            dve_features(dve, c, "2", work, gs2)
            dve.wait_ge(sem("att_in"), 16)
            for h in range(HEADS):
                for which, dst in ((0, s_col[:, h:h + 1]), (1, k3s[:, F + h:F + h + 1])):
                    c.wait(dve)
                    c.up(nc.vector.tensor_tensor_reduce(work[:, 3, 0:FH], k3s[:, h * FH:(h + 1) * FH],
                                                        work[:, 2, h * F + which * FH:h * F + (which + 1) * FH],
                                                        1.0, 0.0, ALU.mult, ALU.add, dst))
            c.wait(dve)
            nc.vector.memset(zero_col, 0.0).then_inc(sem("att"), 1)
            dve.sem_inc(sem("agg2_used"), 2)
            with looped(dve, T // 2, (c, 6)) as b:
                for u in range(2):
                    i = b * 2 + u
                    a = work[:, u, 0:F]
                    dve.wait_ge(sem("agg2"), i + 1)
                    nc.vector.tensor_reduce(a, ps[:, u, 0:3 * F].rearrange("p (s f) -> p f s", s=3), AX_X, ALU.add
                                            ).then_inc(sem("agg2_used"), 1)
                    dve.wait_ge(sem("agg2_used"), i + 3)
                    c.up(nc.vector.scalar_tensor_tensor(a, a, col(degs, i), b2s[:], ALU.mult, ALU.add))
                    c.wait(dve)
                    c.up(nc.vector.scalar_tensor_tensor(tile(xr, i), a, 0.0, tile(xr, i), ALU.max, ALU.add))
                    moments(dve, c, xr, [i])
            c.wait(dve)

            dve_front(dve, c, "3", xr, work)
            for t in range(T):
                d = spread(adj8[:, t, :], t)
                c.up(nc.vector.tensor_tensor(d, d, ident[:], ALU.subtract, saturate=False))
            dve.wait_ge(sem("cp"), 2 + T // 2)
            c.up(nc.vector.memset(cp[:, :, :, FH], 1.0))
            tv = tneigh.rearrange("p t h -> p h t")
            c.up(nc.vector.tensor_reduce(trange[:, 0:2], tv, AX_X, ALU.max))
            c.up(nc.vector.tensor_reduce(trange[:, 2:4], tv, AX_X, ALU.min))
            c.wait(dve)
            nc.vector.tensor_scalar(trange[:, 2:4], trange[:, 2:4], -1.0, None, ALU.mult).then_inc(sem("trange"), 1)
            dve.wait_ge(sem("trange_all"), 1)
            c.up(nc.vector.tensor_tensor(tstep, trange[:, 4:6], trange[:, 6:8], ALU.add))
            c.up(nc.vector.tensor_scalar(tmin, trange[:, 6:8], -1.0, None, ALU.mult))
            c.wait(dve)
            c.up(nc.vector.tensor_tensor(range_max, tstep[:, 0:1], tstep[:, 1:2], ALU.max))
            c.wait(dve)
            nc.vector.tensor_scalar(wide, range_max, SAFE, None, ALU.is_gt).then_inc(sem("wide"), 1)
            c.up(nc.vector.tensor_scalar(tstep, tstep, 1.0 / GRID, None, ALU.mult))
            c.wait(dve)
            for h in range(HEADS):
                c.up(nc.vector.tensor_scalar(theta[:, h, :], grid[:], tstep[:, h:h + 1], tmin[:, h:h + 1],
                                             ALU.mult, ALU.add))
            c.wait(dve)
            for t in range(T):
                for h in range(HEADS):
                    c.up(nc.vector.tensor_scalar(ind[:, t, :][:, h * GRID:(h + 1) * GRID], theta[:, h, :],
                                                 tile(tneigh, t)[:, h:h + 1], None, ALU.is_le, saturate=False))
            c.wait(dve)
            nc.vector.memset(zero_col, 0.0).then_inc(sem("ind"), 1)
            for g in range(J):
                dve.wait_ge(sem("cnt"), g + 1)
                c.wait(dve)
                c.up(nc.vector.tensor_scalar(reach, ps[:, g % 2, :], 0.5, None, ALU.is_gt))
                c.wait(dve)
                nc.vector.tensor_reduce(steps[:, 4 * g:4 * g + 4, :], reach.rearrange("p (i h k) -> p i h k", i=4, h=HEADS),
                                        AX_X, ALU.add).then_inc(sem("reach"), 1)
                dve.wait_ge(sem("reach"), g + 1)
            dve.wait_ge(sem("s_ps"), 1)
            s_row, a_row, m_row = (cols[:, r] for r in range(3))
            c.up(nc.vector.tensor_copy(s_row, ps[:, 4, 0:2 * T].rearrange("p (i h) -> p h i", h=HEADS)))
            for h in range(HEADS):
                c.up(nc.vector.tensor_scalar(m_row[:, h, :], steps[:, :, h], tstep[:, h:h + 1], tmin[:, h:h + 1],
                                             ALU.mult, ALU.add))
            c.wait(dve)
            nc.vector.tensor_tensor(m_row, m_row, s_row, ALU.add).then_inc(sem("zmax"), 1)
            dve.wait_ge(sem("ezmax"), 1)
            c.up(nc.vector.tensor_scalar(a_row, a_row, 1.0, -1.0, ALU.min, ALU.add))
            c.wait(dve)
            c.up(nc.vector.tensor_tensor(m_row, m_row, a_row, ALU.max))
            c.wait(dve)
            c.up(nc.vector.tensor_tensor(a_row, s_row, m_row, ALU.subtract))
            c.wait(dve)
            nc.vector.tensor_scalar(m_row, m_row, 1.0, None, ALU.add).then_inc(sem("cols"), 1)
            dve.sem_inc(sem("x3b"), 2)

            def low(j, b, t, u):
                dve.wait_ge(sem("ez3"), j * T + t + 1)
                nc.vector.scalar_tensor_tensor(work3[:, u], work3[:, u], 1.0, rows[:, b, 2], ALU.min, ALU.subtract
                                               ).then_inc(sem("low3"), 1)

            def scores(j, b, t, u):
                wait_reg(dve, sem("low3"), j * T + t + 1)
                for h in range(HEADS):
                    w = work3[:, u, h, :]
                    nc.vector.scalar_tensor_tensor(w, rows[:, b, 1, h, :], tile(tneigh, t)[:, h:h + 1], w,
                                                   ALU.add, ALU.max).then_inc(sem(f"score3_{h}"), 1)

            def finish(j, b):
                for h in range(HEADS):
                    wait_reg(dve, sem(f"pv3_{h}"), j * T + T + 4)
                for h in range(HEADS):
                    o = h * (CP_W + FH + 1)
                    ins = nc.vector.reciprocal(rinv if h == 0 else rinv2, ps[:, 4 * b:4 * b + 4, o + FH])
                c.up(ins)
                c.wait(dve)
                for s in range(4):
                    for h in range(HEADS):
                        o = h * (CP_W + FH + 1)
                        xt = tile(xr, j * 4 + s)[:, h * FH:(h + 1) * FH]
                        r = (rinv if h == 0 else rinv2)[:, s:s + 1]
                        ins = nc.vector.scalar_tensor_tensor(xt, ps[:, 4 * b + s, o:o + FH], r, xt, ALU.mult, ALU.add)
                ins.then_inc(sem("x3b"), 1)

            def block3(j, b, first=False, last=False):
                for u in range(4):
                    low(j, b, u + 1, (u + 1) % 4)
                    scores(j, b, u, u)
                if not first:
                    finish(j - 1, 1 - b)
                with dve.Fori(1, T // 4 - 1) as tt:
                    for u in range(4):
                        low(j, b, tt * 4 + u + 1, (u + 1) % 4)
                        scores(j, b, tt * 4 + u, u)
                for u in range(4):
                    if u < 3:
                        low(j, b, T - 3 + u, u + 1)
                    elif not last:
                        low(j + 1, 1 - b, 0, 0)
                    scores(j, b, T - 4 + u, u)

            low(0, 0, 0, 0)
            block3(0, 0, first=True)
            with looped(dve, J // 2 - 1, (c, 2)) as j2:
                for b in (1, 0):
                    block3(j2 * 2 + 2 - b, b)
            block3(J - 1, 1, last=True)
            finish(J - 1, 1)
            dve.wait_ge(sem("x3b"), 2 + J)
            nc.vector.memset(zero_col, 0.0).then_inc(sem("x3"), 1)


def kernel(**inputs):
    import numpy as _np
    import concourse.bacc as _bacc
    from concourse import mybir as _mybir
    from concourse.bass_utils import run_bass_kernel_spmd as _run

    nc = _bacc.Bacc("TRN2", target_bir_lowering=False, num_devices=1)
    arrays = {
        "x_in": inputs["x"],
        "adj_t": _np.asarray(inputs["adj"]).T,
        "w0": inputs["L0_gnn_weight"],
        "b0": inputs["L0_gnn_bias"],
        "beta": inputs["L1_gnn_beta"],
        "w2t": _np.asarray(inputs["L2_gnn_W"]).T,
        "b2": inputs["L2_gnn_b"],
        "k3": inputs["L3_gnn_kernels"],
        "att": inputs["L3_gnn_att_kernels"],
    }
    arrays = {n: _np.ascontiguousarray(a) for n, a in arrays.items()}
    args = [nc.dram_tensor(n, a.shape, _mybir.dt.from_np(a.dtype), kind="ExternalInput").ap()
            for n, a in arrays.items()]
    out = nc.dram_tensor("out_0", (4096, 128), _mybir.dt.float32, kind="ExternalOutput").ap()
    build(nc, *args, out)
    r = _run(nc, [arrays], core_ids=[0])
    return r.results[0]["out_0"]
```
